# Optimizing a Trainium2 kernel written in Bass

```python
import numpy as np
import jax
import jax.numpy as jnp

def _softmax(x, axis=-1):
    return jax.nn.softmax(x, axis=axis)

def _gelu(x):
    return jax.nn.gelu(x, approximate=True)

def _silu(x):
    return jax.nn.silu(x)

def _sigmoid(x):
    return jax.nn.sigmoid(x)

def _layernorm(x, axis=-1, eps=1e-05):
    m = jnp.mean(x, axis=axis, keepdims=True)
    v = jnp.var(x, axis=axis, keepdims=True)
    return (x - m) / jnp.sqrt(v + eps)

def _scatter_add(tgt, idx, src, axis=0):
    return tgt.at[idx].add(src)

def _segment_sum(src, seg, n):
    return jax.ops.segment_sum(src, seg, n)
kernel_name = 'mk_xattn_ffn_d1_seqx_r4_565cb6'

def setup_inputs(seed: int=0):
    np.random.seed(seed)
    _w = jnp.asarray

    def _rec_inputs():
        import jax
        import jax.numpy as jnp
        _rk = jax.random.key(seed)
        x = -0.0002928 + 1 * jax.random.normal(jax.random.fold_in(_rk, 1), (8, 256, 256), jnp.float32)
        _lenS = 256 - jax.random.randint(jax.random.fold_in(_rk, 7), (8,), 0, max(1, 256 // 4) + 1, jnp.int32)
        _lenS2 = 256 - jax.random.randint(jax.random.fold_in(_rk, 8), (8,), 0, max(1, 256 // 4) + 1, jnp.int32)
        _ctx_1024P = jax.random.normal(jax.random.fold_in(_rk, 11), (8, 16, 256), jnp.float32)
        _ctx_1024c = jax.random.dirichlet(jax.random.fold_in(_rk, 511), 0.3 * jnp.ones((16,), jnp.float32), (8, 256))
        _ctx_1024t = jnp.einsum('bsk,bkd->bsd', _ctx_1024c, _ctx_1024P)
        _ctx_1024t = _ctx_1024t * jax.lax.rsqrt(jnp.mean(jnp.square(_ctx_1024t)) + 1e-12) * 0.953939
        ctx_1024 = 4.13588e-05 + 0.999923 * (_ctx_1024t + 0.3 * jax.random.normal(jax.random.fold_in(_rk, 611), (8, 256, 256), jnp.float32))
        return (x, ctx_1024)
    x, ctx_1024 = _rec_inputs()

    def _L0_xattn_setup():
        import jax, jax.numpy as jnp
        import numpy as np
        DIM = 256
        NUM_HEADS = 16
        DIM_HEAD = 64
        INNER = NUM_HEADS * DIM_HEAD
        SCALE = DIM_HEAD ** (-0.5)

        def _layernorm(x, gamma, beta, eps=1e-05):
            mu = jnp.mean(x, axis=-1, keepdims=True)
            var = jnp.mean(jnp.square(x - mu), axis=-1, keepdims=True)
            return (x - mu) * jax.lax.rsqrt(var + eps) * gamma + beta
        key = jax.random.key(seed)
        ks = jax.random.split(key, 8)
        B, SQ, SK = (2, 512, 1024)
        x = jax.random.normal(ks[0], (B, SQ, DIM), dtype=jnp.float32)
        context = jax.random.normal(ks[1], (B, SK, DIM), dtype=jnp.float32)
        ln_gamma = jnp.ones((DIM,), jnp.float32)
        ln_beta = jnp.zeros((DIM,), jnp.float32)
        w_q = jax.random.normal(ks[2], (DIM, INNER), dtype=jnp.float32) / np.sqrt(DIM)
        w_kv = jax.random.normal(ks[3], (DIM, 2 * INNER), dtype=jnp.float32) / np.sqrt(DIM)
        w_out = jax.random.normal(ks[4], (INNER, DIM), dtype=jnp.float32) / np.sqrt(INNER)
        b_out = jnp.zeros((DIM,), jnp.float32)
        gate = jnp.array([0.5], jnp.float32)
        return {'x': x, 'context': context, 'ln_gamma': ln_gamma, 'ln_beta': ln_beta, 'w_q': w_q, 'w_kv': w_kv, 'w_out': w_out, 'b_out': b_out, 'gate': gate}
    _L0_xattn_all = _L0_xattn_setup()
    _L0_xattn_in = {k: v for k, v in _L0_xattn_all.items() if k in ('ln_gamma', 'ln_beta', 'w_q', 'w_kv', 'w_out', 'b_out', 'gate')}
    del _L0_xattn_all

    def _L0_ffn_setup():
        import jax, jax.numpy as jnp
        import numpy as np
        NUM_EXPERTS = 4
        key = jax.random.key(seed)
        ks = jax.random.split(key, 8)
        B, L, H = (8, 512, 256)
        F = 4 * H
        s = 0.02
        x = jax.random.normal(ks[0], (B, L, H), dtype=jnp.float32)
        Wr = jax.random.normal(ks[1], (H, NUM_EXPERTS), dtype=jnp.float32) * s
        br = jnp.zeros((NUM_EXPERTS,), dtype=jnp.float32)
        We1 = jax.random.normal(ks[2], (NUM_EXPERTS, H, F), dtype=jnp.float32) * s
        be1 = jnp.zeros((NUM_EXPERTS, F), dtype=jnp.float32)
        We2 = jax.random.normal(ks[3], (NUM_EXPERTS, F, H), dtype=jnp.float32) * s
        be2 = jnp.zeros((NUM_EXPERTS, H), dtype=jnp.float32)
        return {'x': x, 'Wr': Wr, 'br': br, 'We1': We1, 'be1': be1, 'We2': We2, 'be2': be2}
    _L0_ffn_all = _L0_ffn_setup()
    _L0_ffn_in = {k: v for k, v in _L0_ffn_all.items() if k in ('Wr', 'br', 'We1', 'be1', 'We2', 'be2')}
    del _L0_ffn_all
    return {'x': x, 'ctx_1024': ctx_1024, 'L0_xattn_ln_gamma': _L0_xattn_in['ln_gamma'], 'L0_xattn_ln_beta': _L0_xattn_in['ln_beta'], 'L0_xattn_w_q': _L0_xattn_in['w_q'], 'L0_xattn_w_kv': _L0_xattn_in['w_kv'], 'L0_xattn_w_out': _L0_xattn_in['w_out'], 'L0_xattn_b_out': _L0_xattn_in['b_out'], 'L0_xattn_gate': _L0_xattn_in['gate'], 'L0_ffn_Wr': _L0_ffn_in['Wr'], 'L0_ffn_br': _L0_ffn_in['br'], 'L0_ffn_We1': _L0_ffn_in['We1'], 'L0_ffn_be1': _L0_ffn_in['be1'], 'L0_ffn_We2': _L0_ffn_in['We2'], 'L0_ffn_be2': _L0_ffn_in['be2']}

def reference(x, ctx_1024, L0_xattn_ln_gamma, L0_xattn_ln_beta, L0_xattn_w_q, L0_xattn_w_kv, L0_xattn_w_out, L0_xattn_b_out, L0_xattn_gate, L0_ffn_Wr, L0_ffn_br, L0_ffn_We1, L0_ffn_be1, L0_ffn_We2, L0_ffn_be2):
    import jax
    import jax.numpy as jnp

    def _L0_xattn_ref(x, context, ln_gamma, ln_beta, w_q, w_kv, w_out, b_out, gate):
        import jax, jax.numpy as jnp
        import numpy as np
        DIM = 256
        NUM_HEADS = 16
        DIM_HEAD = 64
        INNER = NUM_HEADS * DIM_HEAD
        SCALE = DIM_HEAD ** (-0.5)

        def _layernorm(x, gamma, beta, eps=1e-05):
            mu = jnp.mean(x, axis=-1, keepdims=True)
            var = jnp.mean(jnp.square(x - mu), axis=-1, keepdims=True)
            return (x - mu) * jax.lax.rsqrt(var + eps) * gamma + beta
        B, SQ, _ = x.shape
        SK = context.shape[1]
        xn = _layernorm(x, ln_gamma, ln_beta)
        q = (xn @ w_q).reshape(B, SQ, NUM_HEADS, DIM_HEAD)
        kv = context @ w_kv
        k, v = jnp.split(kv, 2, axis=-1)
        k = k.reshape(B, SK, NUM_HEADS, DIM_HEAD)
        v = v.reshape(B, SK, NUM_HEADS, DIM_HEAD)
        scores = jnp.einsum('bqhd,bkhd->bhqk', q * SCALE, k)
        attn = jax.nn.softmax(scores, axis=-1)
        out = jnp.einsum('bhqk,bkhd->bqhd', attn, v).reshape(B, SQ, INNER)
        out = out @ w_out + b_out
        return out * jnp.tanh(gate[0])

    def _L0_ffn_ref(x, Wr, br, We1, be1, We2, be2):
        import jax, jax.numpy as jnp
        import numpy as np
        NUM_EXPERTS = 4
        logits = jnp.einsum('blh,he->ble', x, Wr) + br
        top_expert = jnp.argmax(logits, axis=-1)
        mask = jax.nn.one_hot(top_expert, NUM_EXPERTS, dtype=x.dtype)
        out = jnp.zeros_like(x)
        for e in range(NUM_EXPERTS):
            h1 = jax.nn.relu(jnp.einsum('blh,hf->blf', x, We1[e]) + be1[e])
            oe = jnp.einsum('blf,fh->blh', h1, We2[e]) + be2[e]
            out = out + mask[..., e:e + 1] * oe
        return out
    x = x + _L0_xattn_ref(_layernorm(x, axis=-1), ctx_1024, L0_xattn_ln_gamma, L0_xattn_ln_beta, L0_xattn_w_q, L0_xattn_w_kv, L0_xattn_w_out, L0_xattn_b_out, L0_xattn_gate)
    x = x + _L0_ffn_ref(_layernorm(x, axis=-1), L0_ffn_Wr, L0_ffn_br, L0_ffn_We1, L0_ffn_be1, L0_ffn_We2, L0_ffn_be2)
    return x

_drawn_inputs = setup_inputs


def setup_inputs(seed=0):
    import zlib

    import numpy as np

    out = dict(_drawn_inputs(seed))
    spreads = {'L0_xattn_ln_gamma': (1.0, 0.2),
     'L0_xattn_ln_beta': (0.0, 0.471),
     'L0_xattn_b_out': (0.0, 0.1),
     'L0_ffn_br': (0.0, 0.1),
     'L0_ffn_be1': (0.0, 0.1),
     'L0_ffn_be2': (0.0, 0.1)}
    factors = {}
    for name, (base, spread) in spreads.items():
        noise = np.random.default_rng([zlib.crc32(name.encode()), seed]).standard_normal(out[name].shape)
        drawn = base * np.exp(spread * noise) if base else spread * noise
        out[name] = jnp.asarray(drawn.astype(out[name].dtype))
    for name, factor in factors.items():
        out[name] = (out[name] * factor).astype(out[name].dtype)
    return out
```

```python
import concourse.bass as bass
from concourse import mybir
from contextlib import ExitStack

F32 = mybir.dt.float32
F32R = mybir.dt.float32r
I32 = mybir.dt.int32
U32 = mybir.dt.uint32
ACT = mybir.ActivationFunctionType
ALU = mybir.AluOpType
AX = mybir.AxisListType

B, S, D = 8, 256, 256
H, DH = 16, 64
INNER = H * DH
E, F = 4, 1024
P = 128
EPS = 1e-5
SCALE = DH ** -0.5

HP = H // 2
TB = S // P
NT = B * TB
DC = D // P
FC = F // P
CH = 512
QS = 4
AHEAD = 3
WCH = (3 * D * INNER + INNER * D) // P // CH
CQ, CK, CV, CO = 0, 4, 8, 12
NG = NT + E - 1


def attention_and_routed_ffn(nc, x, ctx, gamma, beta, w_q, w_kv, w_out, b_out, gate,
                             w_rt, b_r, we1, be1, we2, be2, out):
    xs_dram = nc.dram_tensor("expert_rows", (NG * P, D), F32, kind="Internal").ap()
    ys_dram = nc.dram_tensor("expert_results", (NG * P, D), F32, kind="Internal").ap()
    es = ExitStack()
    with es:
        def sem(name):
            return es.enter_context(nc.semaphore(name))

        def keep(name, shape, dt=F32):
            return es.enter_context(nc.sbuf_tensor(name, shape, dt))

        x_all = keep("x_all", [P, NT * D])
        ident = keep("ident", [P, P])
        stats3 = keep("stats3", [P, NT * 2])
        logits = keep("logits", [P, NT * E])
        gamma_c = keep("gamma_c", [P, DC])
        beta_c = keep("beta_c", [P, DC])
        eps_c = keep("eps_c", [P, TB])
        mhalf_c = keep("mhalf_c", [P, TB])
        gate_c = keep("gate_c", [P, 1])
        tanh_c = keep("tanh_c", [P, 1])
        br_c = keep("br_c", [P, E])
        w1_raw = keep("w1_raw", [P, E * DC * F])

        phase_a = ExitStack()

        def a_sb(name, shape, dt=F32):
            return phase_a.enter_context(nc.sbuf_tensor(name, shape, dt))

        w_hi = a_sb("w_hi", [P, WCH * CH], F32R)
        w_lo = a_sb("w_lo", [P, WCH * CH], F32R)
        q_st = a_sb("q_st", [P, QS * 2 * S], F32R)
        k_mv = a_sb("k_mv", [P, QS * 2 * 2 * S], F32R)
        v_sb = a_sb("v_sb", [P, 2 * TB * CH])
        xt_hi = a_sb("xt_hi", [P, 2 * DC * S], F32R)
        xt_lo = a_sb("xt_lo", [P, 2 * DC * S], F32R)
        ct_hi = a_sb("ct_hi", [P, 2 * DC * S], F32R)
        ct_lo = a_sb("ct_lo", [P, 2 * DC * S], F32R)
        c_in = a_sb("c_in", [P, 2 * TB * D])
        p_sb = a_sb("p_sb", [P, 4 * TB * S])
        pt_sb = a_sb("pt_sb", [P, 2 * TB * S])
        o_hi = a_sb("o_hi", [P, HP * S], F32R)
        o_lo = a_sb("o_lo", [P, HP * S], F32R)
        xn = a_sb("xn", [P, TB * D])
        xt_f = a_sb("xt_f", [P, DC * S])
        xf = a_sb("xf", [P, TB * D])
        prod = a_sb("prod", [P, 2 * D])
        wr_b = a_sb("wr_b", [P, E * D])
        bo_b = a_sb("bo_b", [P, D])
        neg_max = a_sb("neg_max", [P, 4 * TB])
        row_sum = a_sb("row_sum", [P, 4 * TB])
        inv_sum = a_sb("inv_sum", [P, 4 * TB])
        bst = a_sb("bst", [P, TB * 6])
        mv = a_sb("mv", [P, TB * 2])
        rstd = a_sb("rstd", [P, TB])
        var_e = a_sb("var_e", [P, TB])
        bst3 = a_sb("bst3", [P, TB * 6])
        mv3 = a_sb("mv3", [P, TB * 2])
        var_e3 = a_sb("var_e3", [P, TB])
        rstd3 = a_sb("rstd3", [P, TB])
        zero_row = a_sb("zero_row", [P, D])
        lg = a_sb("lg", [P, TB * E])

        phase_a.close()

        def f_sb(name, shape, dt=F32):
            return keep(name, shape, dt)

        w2_raw = f_sb("w2_raw", [P, E * FC * D])
        b1_b = f_sb("b1_b", [P, E * F])
        b2_b = f_sb("b2_b", [P, E * D])
        rt = {n: f_sb("rt_" + n, [P, NT * E]) for n in ("eq", "score", "hot", "cnt", "inc", "off", "pos4")}
        top = f_sb("top", [P, NT])
        mxl = f_sb("mxl", [P, NT])
        pos_f = f_sb("pos_f", [P, NT])
        pos_i = f_sb("pos_i", [P, NT], I32)
        ones_nt = f_sb("ones_nt", [P, NT])
        e_w = f_sb("e_w", [P, E])
        n_f = f_sb("n_f", [P, E])
        n_i = f_sb("n_i", [P, E], I32)
        t_i = f_sb("t_i", [P, E], I32)
        t_f = f_sb("t_f", [P, E])
        t_inc = f_sb("t_inc", [P, E])
        base = f_sb("base", [P, E])
        g_io = f_sb("g_io", [P, NG])
        g_ge = f_sb("g_ge", [P, (E - 1) * NG])
        g_ex = f_sb("g_ex", [P, NG])
        g_i = f_sb("g_i", [P, NG], I32)
        upper = f_sb("upper", [P, P])
        ones_pp = f_sb("ones_pp", [P, P])
        xsend = f_sb("xsend", [P, 4 * D])
        xg = f_sb("xg", [P, 2 * D])
        xgt = f_sb("xgt", [P, 2 * DC * P])
        h1 = f_sb("h1", [P, 2 * F])
        h1t = f_sb("h1t", [P, 2 * F])
        y_sb = f_sb("y_sb", [P, 2 * D])
        yb = f_sb("yb", [P, 4 * D])

        banks = [es.enter_context(nc.psum_tensor(f"bank{n}", [P, CH], F32)) for n in range(8)]
        s_ps = banks[0:2]
        t_ps = banks[2:4]
        o_ps = banks[4]
        qk_ps = banks[5]
        m_ps = banks[6:8]
        h_ps = banks[0:2]
        ht_ps = banks[2:4]
        y_ps = banks[4:6]
        xt_ps = banks[6:8]

        x_in, x_rest_in, wq_in, wk_in, wv_in, wo_in, consts_in, gate_in, b1_in = (
            sem(n) for n in ("x_in", "x_rest_in", "wq_in", "wk_in", "wv_in", "wo_in", "consts_in", "gate_in", "b1_in"))
        c_sem = [sem(f"ctx_in{n}") for n in range(2)]
        w1_in, w2_in, zero_out = sem("w1_in"), sem("w2_in"), sem("zero_out")
        consts_set, tanh_done, xb_done = sem("consts_set"), sem("tanh_done"), sem("xb_done")
        whi_done, wlo_done = sem("whi_done"), sem("wlo_done")
        qk_done, qk_hi, qk_lo = sem("qk_done"), sem("qk_hi"), sem("qk_lo")
        dup_done = [sem(f"dup_done{n}") for n in range(QS)]
        s_done, mx_done, exp_done, norm_done = sem("s_done"), sem("mx_done"), sem("exp_done"), sem("norm_done")
        inv_done = sem("inv_done")
        t_done, pt_done, pv_done = sem("t_done"), sem("pt_done"), sem("pv_done")
        oh_done, ol_done = sem("oh_done"), sem("ol_done")
        m_done, m_free = sem("m_done"), sem("m_free")
        var_done, rstd_done, xn_done = sem("var_done"), sem("rstd_done"), sem("xn_done")
        xth_done, xt_done = sem("xth_done"), sem("xt_done")
        cth_done, ct_done = sem("cth_done"), sem("ct_done")
        var3_done, rstd3_done = sem("var3_done"), sem("rstd3_done")
        dve_chain = sem("dve_chain")
        dve_passed = sem("dve_passed")
        pool_chain = sem("pool_chain")
        phase_a_left, pool_ones = sem("phase_a_left"), sem("pool_ones")
        hot_done, rank_done, pos_done, plan_done = sem("hot_done"), sem("rank_done"), sem("pos_done"), sem("plan_done")
        xsend_done, sent = sem("xsend_done"), [sem(f"sent{n}") for n in range(4)]
        xg_in = [sem(f"xg_in{n}") for n in range(2)]
        xgt_ps_done, xgt_done = sem("xgt_ps_done"), sem("xgt_done")
        h_done, h1_done, ht_done, h1t_done = sem("h_done"), sem("h1_done"), sem("ht_done"), sem("h1t_done")
        y_done, ysb_done = sem("y_done"), sem("ysb_done")
        y_out = [sem(f"y_out{n}") for n in range(2)]
        y_back, x2_done, stored = [sem(f"y_back{n}") for n in range(4)], sem("x2_done"), sem("stored")

        block = es.enter_context(nc.Block())

        def wait(eng, s, value):
            if not (isinstance(value, int) and value <= 0):
                eng.wait_ge(s, value)

        JOBS = ("out0", "out1", "v1a", "v1b", "px", "pc", "v0a", "v0b")

        def job(b, name):
            if isinstance(b, int) and b < 0:
                return {"px": 0, "pc": 1, "v0a": 2, "v0b": 3}[name]
            if isinstance(b, int) and b == B:
                return 8 * (B - 1) + 2 + 4 + {"out0": 0, "out1": 1}[name]
            return 8 * b + 2 + JOBS.index(name)

        def parity(name):
            return {"px": 0, "pc": 1}.get(name, 0 if name in ("out0", "v1a", "v0a") else 1)

        assert all(parity(n) == JOBS.index(n) % 2 for n in JOBS)

        def wq_ap(w, dc, hp):
            c = (CQ + 2 * dc) * CH + hp * P
            return w[:, c:c + P]

        def wk_ap(w, dc, hp):
            c = (CK + 2 * dc) * CH + hp * P
            return w[:, c:c + P]

        def wv_ap(w, dc, half):
            c = (CV + 2 * dc + half) * CH
            return w[:, c:c + CH]

        def wo_ap(w, hp):
            c = CO * CH + hp * D
            return w[:, c:c + D]

        def qst(slot, j):
            return q_st[:, (2 * slot + j) * S:(2 * slot + j + 1) * S]

        def kmv(slot, j, part):
            c = ((2 * slot + j) * 2 + part) * S
            return k_mv[:, c:c + S]

        def half(j):
            return slice(DH * j, DH * j + DH)

        def batches(eng_body, eng):
            eng_body(0, 0, 0)
            with eng.Fori(0, (B - 2) // 2) as i:
                eng_body(2 * i + 1, 1, i)
                eng_body(2 * i + 2, 0, i + 1)
            eng_body(B - 1, 1, (B - 1) // 2)

        def is_first(b):
            return isinstance(b, int) and b == 0

        def is_last(b):
            return isinstance(b, int) and b == B - 1

        def expert_tiles(stage, eng):
            stage(0, 0, 0, False)
            stage(1, 1, 0, False)
            with eng.Fori(1, NG // 2) as i:
                stage(2 * i, 0, i, False)
                stage(2 * i + 1, 1, i, False)
            assert NG % 2
            stage(NG - 1, 0, NG // 2, True)

        @block.sync
        def _(sp):
            sp.dma_start(x_all[:, 0:TB * D].rearrange("p (t d) -> p t d", d=D),
                         x[0].rearrange("(t p) d -> p t d", p=P)).then_inc(x_in, 16)
            sp.dma_start(c_in[:, 0:TB * D].rearrange("p (t d) -> p t d", d=D),
                         ctx[0].rearrange("(t p) d -> p t d", p=P)).then_inc(c_sem[0], 16)
            raw = w1_raw
            sp.dma_start(raw[:, CQ * CH:CK * CH].rearrange("p (c n) -> p c n", c=DC),
                         w_q.rearrange("(c p) n -> p c n", p=P)).then_inc(wq_in, 16)
            sp.dma_start(gamma_c[:, :], gamma).then_inc(consts_in, 16)
            sp.dma_start(beta_c[:, :], beta).then_inc(consts_in, 16)
            kv = w_kv.rearrange("(c p) (s n) -> s p c n", p=P, s=2)
            sp.dma_start(raw[:, CK * CH:CV * CH].rearrange("p (c n) -> p c n", c=DC), kv[0]).then_inc(wk_in, 16)
            sp.dma_start(raw[:, CV * CH:CO * CH].rearrange("p (c n) -> p c n", c=DC), kv[1]).then_inc(wv_in, 16)
            sp.dma_start(raw[:, CO * CH:WCH * CH].rearrange("p (c n) -> p c n", c=HP),
                         w_out.rearrange("(c p) n -> p c n", p=P)).then_inc(wo_in, 16)
            sp.dma_start(gate_c[:, :], gate.partition_broadcast(P)).then_inc(gate_in, 16)
            sp.dma_start(bo_b[:, :], b_out.partition_broadcast(P)).then_inc(gate_in, 16)
            sp.dma_start(br_c[:, :], b_r.partition_broadcast(P)).then_inc(gate_in, 16)
            sp.dma_start(wr_b[:, :], w_rt.rearrange("e d -> (e d)").partition_broadcast(P)).then_inc(gate_in, 16)
            sp.dma_start(x_all[:, TB * D:].rearrange("p (t d) -> p t d", d=D),
                         x[1:].rearrange("b (t p) d -> p (b t) d", p=P)).then_inc(x_rest_in, 16)
            sp.dma_start(c_in[:, TB * D:].rearrange("p (t d) -> p t d", d=D),
                         ctx[1].rearrange("(t p) d -> p t d", p=P)).then_inc(c_sem[1], 16)
            sp.wait_ge(consts_set, 1)
            sp.dma_start(xs_dram.rearrange("(g p) d -> p g d", p=P),
                         zero_row[:, :].unsqueeze(1).broadcast_to((P, NG, D))).then_inc(zero_out, 16)

            def dup(u, slot):
                sp.wait_ge(qk_lo, u + 1)
                for j in range(2):
                    c = (2 * slot + j) * 2 * S
                    sp.dma_start(k_mv[half(1 - j), c:c + 2 * S].bitcast(F32),
                                 k_mv[half(j), c:c + 2 * S].bitcast(F32)).then_inc(dup_done[slot], 16)

            dup(0, 0)
            dup(1, 1)

            def body(b, p):
                u0 = 8 * b
                for hp in range(HP):
                    if not is_last(b) or hp + 2 < HP:
                        dup(u0 + hp + 2, (HP * p + hp + 2) % QS)
                    if is_first(b) and hp == 2:
                        sp.wait_ge(wlo_done, WCH)
                        sp.dma_start(w1_raw[:, :].rearrange("p (ec n) -> p ec n", n=F),
                                     we1.rearrange("e (c p) n -> p (e c) n", p=P)).then_inc(w1_in, 16)
                    if hp == 5 and not is_last(b):
                        sp.wait_ge(m_done, job(b, "pc") + 1)
                        nb = b + 2
                        if isinstance(b, int):
                            src = ctx[nb] if nb < B else None
                        else:
                            src = ctx[bass.ds(nb, 1)].rearrange("o r d -> (o r) d")
                        if src is not None:
                            sp.dma_start(c_in[:, p * TB * D:(p + 1) * TB * D].rearrange("p (t d) -> p t d", d=D),
                                         src.rearrange("(t p) d -> p t d", p=P)).then_inc(c_sem[p], 16)

            body(0, 0)
            with sp.Fori(0, (B - 2) // 2 - 1) as i:
                body(2 * i + 1, 1)
                body(2 * i + 2, 0)
            body(B - 3, 1)
            body(B - 2, 0)
            body(B - 1, 1)

            sp.wait_ge(ol_done, B * HP)
            sp.wait_ge(m_free, job(B, "out1") + 1)
            sp.wait_ge(exp_done, 2 * B * HP)
            sp.wait_ge(phase_a_left, 1)
            sp.dma_start(w2_raw[:, :].rearrange("p (ec n) -> p ec n", n=D),
                         we2.rearrange("e (c p) n -> p (e c) n", p=P)).then_inc(w2_in, 16)
            sp.dma_start(b1_b[:, :], be1.rearrange("e n -> (e n)").partition_broadcast(P)).then_inc(b1_in, 16)
            sp.dma_start(b2_b[:, :], be2.rearrange("e n -> (e n)").partition_broadcast(P)).then_inc(b1_in, 16)

            for n in range(4):
                sp.wait_ge(sent[n], 16 * (NT // 4))

            def load_rows(n, par):
                row = n * P
                src = xs_dram[row:row + P, :] if isinstance(n, int) else xs_dram[bass.ds(row, P), :]
                sp.dma_start(xg[:, par * D:(par + 1) * D], src).then_inc(xg_in[par], 16)

            def store_rows(n, par):
                sp.wait_ge(ysb_done, n + 1)
                row = n * P
                dst = ys_dram[row:row + P, :] if isinstance(n, int) else ys_dram[bass.ds(row, P), :]
                sp.dma_start(dst, y_sb[:, par * D:(par + 1) * D]).then_inc(y_out[par], 16)

            load_rows(0, 0)
            load_rows(1, 1)
            with sp.Fori(0, NG // 2 - 1) as i:
                for par in range(2):
                    n = 2 * i + par
                    sp.wait_ge(xgt_ps_done, n + 1)
                    load_rows(n + 2, par)
                    store_rows(n, par)
            for n in range(2 * (NG // 2 - 1), NG):
                if n + 2 < NG:
                    sp.wait_ge(xgt_ps_done, n + 1)
                    load_rows(n + 2, n % 2)
                store_rows(n, n % 2)

            for t in range(NT):
                sp.wait_ge(x2_done, t + 1)
                sp.dma_start(out[t // TB, (t % TB) * P:(t % TB + 1) * P, :],
                             x_all[:, t * D:(t + 1) * D]).then_inc(stored, 16)
            sp.wait_ge(stored, 16 * NT)

        @block.gpsimd
        def _(pool):
            g = nc.gpsimd
            count = [0]

            def link(ins):
                count[0] += 1
                ins.then_inc(pool_chain, 1)
                pool.wait_ge(pool_chain, count[0])

            g.memset(zero_row[:, :], 0.0).then_inc(consts_set, 1)
            g.memset(eps_c[:, :], EPS)
            g.memset(mhalf_c[:, :], -0.5)
            link(g.memset(ident[:, :], 0.0))
            g.affine_select(out=ident[:, :], in_=ident[:, :], compare_op=ALU.not_equal, fill=1.0, base=0,
                            pattern=[[-1, P]], channel_multiplier=1).then_inc(consts_set, 1)

            def rstd_step(src, tmp, dst, ready, value, done):
                wait(pool, ready, value)
                link2(g.tensor_tensor(tmp[:, :], src[:, 1:2 * TB:2], eps_c[:, :], ALU.add))
                g.tensor_tensor(dst[:, :], tmp[:, :], mhalf_c[:, :], ALU.pow).then_inc(done, 1)

            def add_b_out(b):
                pool.wait_ge(xn_done, b + 1)
                n = TB * D
                xb = x_all[:, b * n:b * n + n] if isinstance(b, int) else x_all[:, bass.ds(b * n, n)]
                xb = xb.rearrange("p (t d) -> p t d", t=TB)
                g.tensor_tensor(xb, xb, bo_b[:, :].unsqueeze(1).broadcast_to((P, TB, D)), ALU.add).then_inc(xb_done, 1)

            def normalise(u, par, j):
                pool.wait_ge(inv_done, 2 * u + j + 1)
                slot = 2 * par + j
                pv = p_sb[:, slot * TB * S:(slot + 1) * TB * S].rearrange("p (t k) -> p t k", t=TB)
                rs = inv_sum[:, slot * TB:(slot + 1) * TB].unsqueeze(2).broadcast_to((P, TB, S))
                g.tensor_tensor(pv, pv, rs, ALU.mult).then_inc(norm_done, 1)

            chain = {"base": count[0], "n": 0}
            PER_BATCH = 3

            def link2(ins):
                chain["n"] += 1
                ins.then_inc(pool_chain, 1)
                pool.wait_ge(pool_chain, chain["base"] + chain["n"])

            pool.wait_ge(consts_set, 2)
            rstd_step(mv, var_e, rstd, var_done, 1, rstd_done)
            rstd_step(mv, var_e, rstd, var_done, 2, rstd_done)
            pool.wait_ge(tanh_done, 1)
            pool.wait_ge(gate_in, 64)
            link2(g.tensor_scalar(bo_b[:, :], bo_b[:, :], tanh_c[:, 0:1], None, ALU.mult))
            base0 = chain["base"] + chain["n"]
            normalise(0, 0, 0)
            normalise(0, 0, 1)

            def body(b, p, b_half):
                first, last = is_first(b), is_last(b)
                chain["base"], chain["n"] = base0 if first else base0 + 2 + PER_BATCH * (b - 1), 0
                u0 = 8 * b
                for hp in range(HP):
                    if hp in (0, 1) and not last:
                        rstd_step(mv, var_e, rstd, var_done, 2 * b + 3 + hp, rstd_done)
                    if not (last and hp == HP - 1):
                        for j in range(2):
                            normalise(u0 + hp + 1, (hp + 1) % 2, j)
                    if hp == 3 and not first:
                        rstd_step(mv3, var_e3, rstd3, var3_done, b, rstd3_done)
                    if hp == 5:
                        add_b_out(b)

            batches(body, pool)
            chain["base"], chain["n"] = base0 + 2 + PER_BATCH * (B - 2) + 1, 0
            rstd_step(mv3, var_e3, rstd3, var3_done, B, rstd3_done)

            pool.wait_ge(ol_done, B * HP)
            pool.wait_ge(m_free, job(B, "out1") + 1)
            pool.wait_ge(phase_a_left, 1)
            g.memset(ones_nt[:, :], 1.0)
            g.iota(g_io[:, :], [[1, NG]], base=0, channel_multiplier=0, allow_small_or_imprecise_dtypes=True)
            g.iota(e_w[:, :], [[-1, E]], base=E, channel_multiplier=0, allow_small_or_imprecise_dtypes=True)
            g.memset(ones_pp[:, :], 1.0).then_inc(pool_ones, 1)
            pool.wait_ge(pool_ones, 1)
            g.affine_select(out=upper[:, :], in_=ones_pp[:, :], compare_op=ALU.is_gt, fill=0.0, base=0,
                            pattern=[[1, P]], channel_multiplier=-1).then_inc(consts_set, 1)

            pool.wait_ge(pos_done, 1)
            pool.wait_ge(zero_out, 16)
            for t in range(NT):
                pool.wait_ge(xsend_done, t + 1)
                g.indirect_dma_start(out=xs_dram[:, :],
                                     out_offset=bass.IndirectOffsetOnAxis(ap=pos_i[:, t:t + 1].bitcast(U32), axis=0),
                                     in_=xsend[:, (t % 4) * D:(t % 4 + 1) * D], in_offset=None).then_inc(sent[t % 4], 16)
            for n in range(2):
                pool.wait_ge(y_out[n], 16 * ((NG + 1 - n) // 2))
            for t in range(NT):
                if t >= 4:
                    pool.wait_ge(x2_done, t - 3)
                g.indirect_dma_start(out=yb[:, (t % 4) * D:(t % 4 + 1) * D], out_offset=None,
                                     in_=ys_dram[:, :],
                                     in_offset=bass.IndirectOffsetOnAxis(ap=pos_i[:, t:t + 1].bitcast(U32), axis=0)
                                     ).then_inc(y_back[t % 4], 16)

        @block.scalar
        def _(act):
            a = nc.scalar

            def split_hi(c, arrived):
                if arrived is not None:
                    act.wait_ge(arrived, 16)
                a.activation(w_hi[:, c * CH:(c + 1) * CH], w1_raw[:, c * CH:(c + 1) * CH],
                             ACT.Copy).then_inc(whi_done, 1)

            def ctx_hi(b, jb, par):
                act.wait_ge(m_done, jb + 1)
                a.activation(ct_hi[:, par * DC * S:(par + 1) * DC * S], m_ps[1][:, :],
                             ACT.Copy).then_inc(cth_done, 1)

            def x_hi(jb, par):
                act.wait_ge(m_free, jb + 1)
                a.activation(xt_hi[:, par * DC * S:(par + 1) * DC * S], xt_f[:, :], ACT.Copy).then_inc(xth_done, 1)

            def qk_high(u, slot):
                act.wait_ge(qk_done, u + 1)
                for j in range(2):
                    a.activation(qst(slot, j)[half(j), :], qk_ps[half(j), 0:S], ACT.Copy, scale=SCALE)
                for j in range(2):
                    last = a.activation(kmv(slot, j, 0)[half(j), :], qk_ps[half(j), S:2 * S], ACT.Copy)
                last.then_inc(qk_hi, 1)

            def exponentials(u, par, j):
                act.wait_ge(mx_done, 2 * u + j + 1)
                wait(act, t_done, 2 * (u - 2) + j + 1)
                slot = 2 * par + j
                for t in range(TB):
                    last = a.activation(p_sb[:, (slot * TB + t) * S:(slot * TB + t + 1) * S],
                                        s_ps[j][:, t * S:(t + 1) * S], ACT.Exp,
                                        bias=neg_max[:, slot * TB + t:slot * TB + t + 1],
                                        accum_out=row_sum[:, slot * TB + t:slot * TB + t + 1])
                last.then_inc(exp_done, 1)

            def evacuate_pt(u, j):
                act.wait_ge(t_done, 2 * u + j + 1)
                a.activation(pt_sb[:, j * TB * S:(j + 1) * TB * S], t_ps[j][:, :], ACT.Copy).then_inc(pt_done, 1)

            def out_high(u, hp, b):
                act.wait_ge(pv_done, u + 1)
                if not is_first(b):
                    wait(act, m_done, job(b, "out1") + 1)
                a.activation(o_hi[:, hp * S:(hp + 1) * S], o_ps[:, 0:S], ACT.Copy).then_inc(oh_done, 1)

            for c in range(CQ, CV):
                split_hi(c, {CQ: wq_in, CK: wk_in}.get(c))
            ctx_hi(0, job(-1, "pc"), 0)
            x_hi(job(-1, "px"), 0)
            for c in range(CV, CO):
                split_hi(c, {CV: wv_in}.get(c))
            qk_high(0, 0)
            qk_high(1, 1)
            act.wait_ge(gate_in, 64)
            a.activation(tanh_c[:, :], gate_c[:, :], ACT.Tanh).then_inc(tanh_done, 1)
            exponentials(0, 0, 0)
            exponentials(0, 0, 1)
            qk_high(2, 2)
            for c in range(CO, WCH):
                split_hi(c, {CO: wo_in}.get(c))

            def body(b, p, b_half):
                u0 = 8 * b
                last = is_last(b)
                for hp in range(HP):
                    u = u0 + hp
                    if hp > 0:
                        out_high(u - 1, hp - 1, b)
                    elif not is_first(b):
                        out_high_prev(u - 1, b)
                    evacuate_pt(u, 0)
                    evacuate_pt(u, 1)
                    if not (last and hp == HP - 1):
                        exponentials(u + 1, (hp + 1) % 2, 0)
                        exponentials(u + 1, (hp + 1) % 2, 1)
                    if not last or hp + AHEAD < HP:
                        qk_high(u + AHEAD, (HP * p + hp + AHEAD) % QS)
                    if hp == 3 and not last:
                        ctx_hi(b + 1, job(b, "pc"), 1 - p)
                        x_hi(job(b, "px"), 1 - p)

            def out_high_prev(u, b):
                act.wait_ge(pv_done, u + 1)
                prev = b - 1
                if not (isinstance(prev, int) and prev <= 0):
                    wait(act, m_done, job(prev, "out1") + 1)
                a.activation(o_hi[:, (HP - 1) * S:HP * S], o_ps[:, 0:S], ACT.Copy).then_inc(oh_done, 1)

            batches(body, act)
            out_high_prev(B * HP - 1, B)

            def xg_evacuate(n, par):
                act.wait_ge(xgt_ps_done, n + 1)
                a.activation(xgt[:, par * DC * P:(par + 1) * DC * P], xt_ps[par][:, 0:DC * P],
                             ACT.Copy).then_inc(xgt_done, 1)

            act.wait_ge(phase_a_left, 1)
            act.wait_ge(m_free, job(B, "out1") + 1)
            xg_evacuate(0, 0)

            def stage(n, par, n_half, last):
                if not last:
                    xg_evacuate(n + 1, 1 - par)
                for c in range(2):
                    act.wait_ge(ht_done, 2 * n + c + 1)
                    a.activation(h1t[:, par * F + c * CH:par * F + (c + 1) * CH], ht_ps[c][:, :],
                                 ACT.Relu).then_inc(h1t_done, 1)

            expert_tiles(stage, act)

        @block.vector
        def _(dve):
            v = nc.vector
            chain = {"base": 0, "n": 0}

            def link(ins):
                chain["n"] += 1
                ins.then_inc(dve_chain, 1)
                dve.wait_ge(dve_chain, chain["base"] + chain["n"])

            def x_tile(b, t):
                if isinstance(b, int):
                    c = (TB * b + t) * D
                    return x_all[:, c:c + D]
                return x_all[:, bass.ds((b * TB + t) * D, D)]

            def moments(src, st, dst, done):
                for t in range(TB):
                    last = v.bn_stats(st[:, 6 * t:6 * t + 6], src(t))
                link(last)
                dve.sem_inc(dve_passed, 1)
                for t in range(TB):
                    last = v.bn_aggr(dst[:, 2 * t:2 * t + 2], st[:, 6 * t:6 * t + 6])
                last.then_inc(done, 1)

            def standardise(dst, src, m, r):
                for t in range(TB):
                    last = v.tensor_scalar(dst[:, t * D:(t + 1) * D], src(t), m[:, 2 * t:2 * t + 1],
                                           r[:, t:t + 1], ALU.subtract, ALU.mult)
                return last

            def xn_tile(t):
                return xn[:, t * D:(t + 1) * D]

            def split_lo(c):
                dve.wait_ge(whi_done, c + 1)
                s = slice(c * CH, (c + 1) * CH)
                v.tensor_tensor(w_lo[:, s], w1_raw[:, s], w_hi[:, s].bitcast(F32), ALU.subtract).then_inc(wlo_done, 1)

            def norm_a(b):
                moments(lambda t: x_tile(b, t), bst, mv, var_done)

            def norm_b(b):
                dve.wait_ge(rstd_done, 2 * b + 1)
                link(standardise(xn, lambda t: x_tile(b, t), mv, rstd))
                moments(xn_tile, bst, mv, var_done)

            def norm_c(b):
                dve.wait_ge(rstd_done, 2 * b + 2)
                standardise(xn, xn_tile, mv, rstd).then_inc(xn_done, 1)

            def x_affine(b, jb):
                dve.wait_ge(m_done, jb + 1)
                for c in range(DC):
                    last = v.tensor_scalar(xt_f[:, c * S:(c + 1) * S], m_ps[0][:, c * S:(c + 1) * S],
                                           gamma_c[:, c:c + 1], beta_c[:, c:c + 1], ALU.mult, ALU.add)
                last.then_inc(m_free, 1)

            def x_low(b, par):
                dve.wait_ge(xth_done, b + 1)
                s = slice(par * DC * S, (par + 1) * DC * S)
                v.tensor_tensor(xt_lo[:, s], xt_f[:, :], xt_hi[:, s].bitcast(F32), ALU.subtract).then_inc(xt_done, 1)

            def ctx_low(b, par):
                dve.wait_ge(cth_done, b + 1)
                s = slice(par * DC * S, (par + 1) * DC * S)
                v.tensor_tensor(ct_lo[:, s], m_ps[1][:, :], ct_hi[:, s].bitcast(F32),
                                ALU.subtract).then_inc(m_free, 1)

            def v_evacuate(jb, hf, kt):
                dve.wait_ge(m_done, jb + 1)
                c = (hf * TB + kt) * CH
                v.tensor_copy(v_sb[:, c:c + CH], m_ps[kt][:, :]).then_inc(m_free, 1)

            def residual(b, t, jb):
                dve.wait_ge(m_done, jb + 1)
                dve.wait_ge(xb_done, b + 1)
                v.scalar_tensor_tensor(out=x_tile(b, t), in0=m_ps[t][:, 0:D], scalar=tanh_c[:, 0:1],
                                       in1=x_tile(b, t), op0=ALU.mult, op1=ALU.add).then_inc(m_free, 1)

            def qk_low(u, slot):
                dve.wait_ge(qk_hi, u + 1)
                for j in range(2):
                    v.scalar_tensor_tensor(out=qst(slot, j)[half(1 - j), :], in0=qk_ps[half(j), 0:S], scalar=SCALE,
                                           in1=qst(slot, j)[half(j), :].bitcast(F32), op0=ALU.mult, op1=ALU.subtract)
                for j in range(2):
                    last = v.tensor_tensor(kmv(slot, j, 1)[half(j), :], qk_ps[half(j), S:2 * S],
                                           kmv(slot, j, 0)[half(j), :].bitcast(F32), ALU.subtract)
                last.then_inc(qk_lo, 1)

            def maxima(u, par, j):
                dve.wait_ge(s_done, 2 * u + j + 1)
                slot = 2 * par + j
                v.tensor_reduce(neg_max[:, slot * TB:(slot + 1) * TB],
                                s_ps[j][:, :].rearrange("p (t k) -> p t k", t=TB), AX.X, ALU.max,
                                negate=True).then_inc(mx_done, 1)

            def inverse_sums(u, par, j):
                dve.wait_ge(exp_done, 2 * u + j + 1)
                slot = 2 * par + j
                v.reciprocal(inv_sum[:, slot * TB:(slot + 1) * TB],
                             row_sum[:, slot * TB:(slot + 1) * TB]).then_inc(inv_done, 1)

            def out_low(u, hp):
                dve.wait_ge(oh_done, u + 1)
                s = slice(hp * S, (hp + 1) * S)
                v.tensor_tensor(o_lo[:, s], o_ps[:, 0:S], o_hi[:, s].bitcast(F32), ALU.subtract).then_inc(ol_done, 1)

            def ffn_norm_a(b):
                moments(lambda t: x_tile(b, t), bst3, mv3, var3_done)

            def ffn_norm_b(b):
                dve.wait_ge(rstd3_done, b + 1)
                for t in range(TB):
                    cols = stats_cols(b, t)
                    v.tensor_copy(cols(0), mv3[:, 2 * t:2 * t + 1])
                    v.tensor_copy(cols(1), rstd3[:, t:t + 1])
                link(standardise(xf, lambda t: x_tile(b, t), mv3, rstd3))

            def stats_cols(b, t):
                def at(k):
                    if isinstance(b, int):
                        c = (TB * b + t) * 2 + k
                        return stats3[:, c:c + 1]
                    return stats3[:, bass.ds((b * TB + t) * 2 + k, 1)]
                return at

            def router(t):
                room = [prod[:, 0:D], prod[:, D:2 * D], xt_f[:, 0:D], xt_f[:, D:2 * D]]
                for e in range(E):
                    last = v.tensor_tensor_reduce(out=room[e], in0=xf[:, t * D:(t + 1) * D],
                                                  in1=wr_b[:, e * D:(e + 1) * D], scale=1.0, scalar=0.0,
                                                  op0=ALU.mult, op1=ALU.add, accum_out=lg[:, t * E + e:t * E + e + 1])
                link(last)

            def logits_out(b):
                n = TB * E
                dst = logits[:, n * b:n * b + n] if isinstance(b, int) else logits[:, bass.ds(b * n, n)]
                return v.tensor_tensor(dst.rearrange("p (t e) -> p t e", e=E),
                                       lg[:, :].rearrange("p (t e) -> p t e", e=E),
                                       br_c[:, :].unsqueeze(1).broadcast_to((P, TB, E)), ALU.add)

            dve.wait_ge(x_in, 16)
            norm_a(0)
            norm_b(0)
            norm_c(0)
            dve.wait_ge(consts_in, 32)
            x_affine(0, job(-1, "px"))
            for c in range(CQ, CV):
                split_lo(c)
            ctx_low(0, 0)
            x_low(0, 0)
            dve.wait_ge(x_rest_in, 16)
            for c in range(CV, CO):
                split_lo(c)
            qk_low(0, 0)
            qk_low(1, 1)
            v_evacuate(job(-1, "v0a"), 0, 0)
            v_evacuate(job(-1, "v0b"), 0, 1)
            dve.wait_ge(gate_in, 64)
            maxima(0, 0, 0)
            maxima(0, 0, 1)
            inverse_sums(0, 0, 0)
            inverse_sums(0, 0, 1)
            for c in range(CO, WCH):
                split_lo(c)
            base0 = chain["base"] + chain["n"]
            PER_BATCH = 7

            def body(b, p, b_half):
                first, last = is_first(b), is_last(b)
                chain["base"], chain["n"] = base0 if first else base0 + 3 + PER_BATCH * (b - 1), 0
                u0 = 8 * b
                for hp in range(HP):
                    u = u0 + hp
                    if not last or hp + 2 < HP:
                        qk_low(u + 2, (HP * p + hp + 2) % QS)
                    if not (last and hp == HP - 1):
                        maxima(u + 1, (hp + 1) % 2, 0)
                        maxima(u + 1, (hp + 1) % 2, 1)
                    if not (first and hp == 0):
                        out_low(u - 1, (hp - 1) % HP)
                    if hp == 0 and not last:
                        norm_a(b + 1)
                    if hp == 1 and not last:
                        norm_b(b + 1)
                    if hp == 2 and not last:
                        norm_c(b + 1)
                    if hp in (0, 1) and not first:
                        residual(b - 1, hp, job(b, f"out{hp}"))
                    if hp == 2:
                        v_evacuate(job(b, "v1a"), 1, 0)
                        v_evacuate(job(b, "v1b"), 1, 1)
                        if not first:
                            ffn_norm_a(b - 1)
                    if hp == 3 and not last:
                        x_affine(b + 1, job(b, "px"))
                        ctx_low(b + 1, 1 - p)
                        x_low(b + 1, 1 - p)
                    if hp == 5 and not first:
                        ffn_norm_b(b - 1)
                        router(0)
                    if hp == 6 and not last:
                        v_evacuate(job(b, "v0a"), 0, 0)
                        v_evacuate(job(b, "v0b"), 0, 1)
                    if hp == 7 and not first:
                        router(1)
                        logits_out(b - 1)
                    if not (last and hp == HP - 1):
                        inverse_sums(u + 1, (hp + 1) % 2, 0)
                        inverse_sums(u + 1, (hp + 1) % 2, 1)
                assert chain["n"] == (3 if first else PER_BATCH - 3 if last else PER_BATCH)

            batches(body, dve)
            chain["base"], chain["n"] = base0 + 3 + PER_BATCH * (B - 2) + PER_BATCH - 3, 0
            out_low(B * HP - 1, HP - 1)
            for t in range(TB):
                residual(B - 1, t, job(B, f"out{t}"))
            dve.wait_ge(m_free, job(B, "out1") + 1)
            ffn_norm_a(B - 1)
            ffn_norm_b(B - 1)
            router(0)
            router(1)
            link(logits_out(B - 1))
            dve.wait_ge(zero_out, 16)
            v.tensor_copy(mv3[:, 0:1], rstd3[:, 0:1]).then_inc(phase_a_left, 1)

            dve.wait_ge(consts_set, 3)
            nt_e = lambda tl: tl[:, :].rearrange("p (t e) -> p t e", e=E)
            per_t = lambda tl: tl[:, :].unsqueeze(2).broadcast_to((P, NT, E))
            per_e = lambda tl: tl[:, :].unsqueeze(1).broadcast_to((P, NT, E))
            lg3 = nt_e(logits)
            link(v.tensor_reduce(mxl[:, :], lg3, AX.X, ALU.max))
            link(v.tensor_tensor(nt_e(rt["eq"]), lg3, per_t(mxl), ALU.is_ge))
            link(v.tensor_tensor(nt_e(rt["score"]), nt_e(rt["eq"]), per_e(e_w), ALU.mult))
            link(v.tensor_reduce(top[:, :], nt_e(rt["score"]), AX.X, ALU.max))
            v.tensor_tensor(nt_e(rt["hot"]), per_e(e_w), per_t(top), ALU.is_equal).then_inc(hot_done, 1)
            dve.wait_ge(rank_done, 1)
            link(v.tensor_copy(rt["cnt"][:, :], banks[1][:, 0:NT * E]))
            for e in range(E):
                last = v.tensor_tensor_scan(rt["inc"][:, e::E], ones_nt[:, :], rt["cnt"][:, e::E], 0.0,
                                            ALU.mult, ALU.add)
            link(last)
            link(v.tensor_scalar(n_f[:, :], rt["inc"][:, (NT - 1) * E:NT * E], float(P - 1), None, ALU.add))
            link(v.tensor_copy(n_i[:, :], n_f[:, :]))
            link(v.tensor_scalar(t_i[:, :], n_i[:, :], 7, None, ALU.arith_shift_right))
            link(v.tensor_copy(t_f[:, :], t_i[:, :]))
            link(v.tensor_tensor_scan(t_inc[:, :], ones_nt[:, 0:E], t_f[:, :], 0.0, ALU.mult, ALU.add))
            link(v.tensor_tensor(base[:, :], t_inc[:, :], t_f[:, :], ALU.subtract))
            link(v.tensor_scalar(base[:, :], base[:, :], float(P), None, ALU.mult))
            link(v.tensor_tensor(rt["off"][:, :], rt["inc"][:, :], rt["cnt"][:, :], ALU.subtract))
            link(v.tensor_tensor(rt["off"][:, :], rt["off"][:, :], banks[0][:, 0:NT * E], ALU.add))
            link(v.tensor_tensor(nt_e(rt["off"]), nt_e(rt["off"]), per_e(base), ALU.add))
            link(v.tensor_tensor(rt["pos4"][:, :], rt["off"][:, :], rt["hot"][:, :], ALU.mult))
            link(v.tensor_reduce(pos_f[:, :], nt_e(rt["pos4"]), AX.X, ALU.add))
            v.tensor_copy(pos_i[:, :], pos_f[:, :]).then_inc(pos_done, 1)
            for e in range(E - 1):
                last = v.tensor_scalar(g_ge[:, e * NG:(e + 1) * NG], g_io[:, :], t_inc[:, e:e + 1], None, ALU.is_ge)
            link(last)
            link(v.tensor_tensor(g_ex[:, :], g_ge[:, 0:NG], g_ge[:, NG:2 * NG], ALU.add))
            link(v.tensor_tensor(g_ex[:, :], g_ex[:, :], g_ge[:, 2 * NG:3 * NG], ALU.add))
            link(v.tensor_copy(g_i[:, :], g_ex[:, :]))
            v.tensor_copy(top[:, 0:1], mxl[:, 0:1]).then_inc(plan_done, 1)
            for t in range(NT):
                if t >= 4:
                    dve.wait_ge(sent[t % 4], 16 * (t // 4))
                v.tensor_scalar(xsend[:, (t % 4) * D:(t % 4 + 1) * D], x_all[:, t * D:(t + 1) * D],
                                stats3[:, 2 * t:2 * t + 1], stats3[:, 2 * t + 1:2 * t + 2],
                                ALU.subtract, ALU.mult).then_inc(xsend_done, 1)

            dve.wait_ge(b1_in, 32)

            def expert_of(n):
                return dve.value_load(g_i[0:1, n:n + 1] if isinstance(n, int) else g_i[0:1, bass.ds(n, 1)],
                                      min_val=0, max_val=E - 1)

            def h_bias(n, par, ex):
                for c in range(2):
                    dve.wait_ge(h_done, 2 * n + c + 1)
                    col = par * F + c * CH
                    v.tensor_tensor(h1[:, col:col + CH], h_ps[c][:, :],
                                    b1_b[:, bass.ds(ex * F + c * CH, CH)], ALU.add).then_inc(h1_done, 1)

            def y_bias(n, par, n_half, ex):
                dve.wait_ge(y_done, n + 1)
                wait(dve, y_out[par], 16 * n_half)
                v.tensor_tensor(y_sb[:, par * D:(par + 1) * D], y_ps[par][:, 0:D],
                                b2_b[:, bass.ds(ex * D, D)], ALU.add).then_inc(ysb_done, 1)

            h_bias(0, 0, expert_of(0))

            def stage(n, par, n_half, last):
                if not last:
                    h_bias(n + 1, 1 - par, expert_of(n + 1))
                y_bias(n, par, n_half, expert_of(n))

            expert_tiles(stage, dve)

            for t in range(NT):
                dve.wait_ge(y_back[t % 4], 16 * (t // 4 + 1))
                v.tensor_tensor(x_all[:, t * D:(t + 1) * D], x_all[:, t * D:(t + 1) * D],
                                yb[:, (t % 4) * D:(t % 4 + 1) * D], ALU.add).then_inc(x2_done, 1)

        @block.tensor
        def _(pe):
            mm = nc.tensor.matmul

            def three(outp, terms):
                n = len(terms)
                for k, (lh, ll, rh, rl) in enumerate(terms):
                    mm(outp, lh, rh, start=(k == 0), stop=False)
                    mm(outp, lh, rl, start=False, stop=False)
                    last = mm(outp, ll, rh, start=False, stop=(k == n - 1))
                return last

            def project_qk(u, hp, par, b):
                wait(pe, qk_lo, u)
                s = [slice((par * DC + c) * S, (par * DC + c + 1) * S) for c in range(DC)]
                three(qk_ps[:, 0:S], [(wq_ap(w_hi, c, hp), wq_ap(w_lo, c, hp), xt_hi[:, s[c]], xt_lo[:, s[c]])
                                      for c in range(DC)])
                three(qk_ps[:, S:2 * S], [(wk_ap(w_hi, c, hp), wk_ap(w_lo, c, hp), ct_hi[:, s[c]], ct_lo[:, s[c]])
                                          for c in range(DC)]).then_inc(qk_done, 1)

            def project_v(jb, hf, kt, par):
                wait(pe, m_free, jb - 1)
                s = [slice((par * DC + c) * S + kt * P, (par * DC + c) * S + (kt + 1) * P) for c in range(DC)]
                three(m_ps[kt][:, :], [(ct_hi[:, s[c]], ct_lo[:, s[c]], wv_ap(w_hi, c, hf), wv_ap(w_lo, c, hf))
                                       for c in range(DC)]).then_inc(m_done, 1)

            def transposes(jb, bank, src):
                wait(pe, m_free, jb - 1)
                for t in range(TB):
                    for c in range(DC):
                        last = nc.tensor.transpose(m_ps[bank][:, c * S + t * P:c * S + (t + 1) * P],
                                                   src[:, t * D + c * P:t * D + (c + 1) * P], ident[:, :])
                last.then_inc(m_done, 1)

            def scores(u, slot, j):
                wait(pe, exp_done, 2 * (u - 1) + j + 1)
                for t in range(TB):
                    q = qst(slot, j)[:, t * P:(t + 1) * P]
                    mm(s_ps[j][:, t * S:(t + 1) * S], q, kmv(slot, j, 0), start=True, stop=False)
                    last = mm(s_ps[j][:, t * S:(t + 1) * S], q, kmv(slot, j, 1), start=False, stop=True)
                last.then_inc(s_done, 1)

            def transpose_p(u, par, j):
                pe.wait_ge(norm_done, 2 * u + j + 1)
                wait(pe, pt_done, 2 * (u - 1) + j + 1)
                slot = 2 * par + j
                for t in range(TB):
                    for kt in range(TB):
                        c = (slot * TB + t) * S + kt * P
                        last = nc.tensor.transpose(t_ps[j][:, kt * S + t * P:kt * S + (t + 1) * P],
                                                   p_sb[:, c:c + P], ident[:, :])
                last.then_inc(t_done, 1)

            def attend(u, hp):
                wait(pe, pt_done, 2 * u + 2)
                wait(pe, ol_done, u)
                hf, q4 = hp // 4, hp % 4
                for kt in range(TB):
                    for j in range(2):
                        c = (hf * TB + kt) * CH + q4 * P + j * DH
                        last = mm(o_ps[half(j), 0:S], v_sb[:, c:c + DH],
                                  pt_sb[:, (j * TB + kt) * S:(j * TB + kt + 1) * S],
                                  start=(kt == 0), stop=(kt == TB - 1))
                last.then_inc(pv_done, 1)

            def project_out(jb, t):
                wait(pe, m_free, jb - 1)
                terms = []
                for hp in range(HP):
                    s = slice(hp * S + t * P, hp * S + (t + 1) * P)
                    terms.append((o_hi[:, s], o_lo[:, s], wo_ap(w_hi, hp), wo_ap(w_lo, hp)))
                three(m_ps[t][:, 0:D], terms).then_inc(m_done, 1)

            pe.wait_ge(consts_set, 2)
            pe.wait_ge(xn_done, 1)
            transposes(job(-1, "px"), 0, xn[:, :])
            pe.wait_ge(c_sem[0], 16)
            transposes(job(-1, "pc"), 1, c_in[:, 0:TB * D])
            pe.wait_ge(wlo_done, CV)
            pe.wait_ge(xt_done, 1)
            pe.wait_ge(m_free, 2)
            for u in range(AHEAD):
                if u == 2:
                    pe.wait_ge(wlo_done, CO)
                    project_v(job(-1, "v0a"), 0, 0, 0)
                    project_v(job(-1, "v0b"), 0, 1, 0)
                    pe.wait_ge(dup_done[0], 32)
                    scores(0, 0, 0)
                    scores(0, 0, 1)
                project_qk(u, u, 0, 0)

            def body(b, p, b_half):
                first, last = is_first(b), is_last(b)
                for hp in range(HP):
                    u = 8 * b + hp
                    if not (last and hp == HP - 1):
                        slot = (HP * p + hp + 1) % QS
                        pe.wait_ge(dup_done[slot], 32 * (b * (HP // QS) + (hp + 1) // QS + 1))
                        scores(u + 1, slot, 0)
                        scores(u + 1, slot, 1)
                    transpose_p(u, hp % 2, 0)
                    transpose_p(u, hp % 2, 1)
                    if not last or hp + AHEAD < HP:
                        nxt = hp + AHEAD >= HP
                        if hp + AHEAD == HP:
                            pe.wait_ge(xt_done, b + 2)
                            pe.wait_ge(m_free, job(b, "pc") + 1)
                        project_qk(u + AHEAD, (hp + AHEAD) % HP, (1 - p) if nxt else p, b)
                    if hp in (0, 1) and not first:
                        if hp == 0:
                            pe.wait_ge(ol_done, u)
                            pe.wait_ge(wlo_done, WCH)
                        project_out(job(b, f"out{hp}"), hp)
                    if hp == 2:
                        project_v(job(b, "v1a"), 1, 0, p)
                        project_v(job(b, "v1b"), 1, 1, p)
                    if hp == 3 and not last:
                        pe.wait_ge(xn_done, b + 2)
                        transposes(job(b, "px"), 0, xn[:, :])
                        pe.wait_ge(c_sem[1 - p], 16 * (b_half + p + 1))
                        transposes(job(b, "pc"), 1, c_in[:, (1 - p) * TB * D:(2 - p) * TB * D])
                    if hp == 6 and not last:
                        project_v(job(b, "v0a"), 0, 0, 1 - p)
                        project_v(job(b, "v0b"), 0, 1, 1 - p)
                    if hp == 0:
                        wait(pe, m_free, job(b - 1, "v0b") + 1)
                    if hp == 4:
                        wait(pe, m_free, job(b, "v1b") + 1)
                    attend(u, hp)

            batches(body, pe)
            pe.wait_ge(ol_done, B * HP)
            project_out(job(B, "out0"), 0)
            project_out(job(B, "out1"), 1)

            pe.wait_ge(hot_done, 1)
            mm(banks[0][:, 0:NT * E], upper[:, :], rt["hot"][:, :], start=True, stop=True)
            mm(banks[1][:, 0:NT * E], ones_pp[:, :], rt["hot"][:, :], start=True, stop=True).then_inc(rank_done, 1)

            def expert_of(n):
                return pe.value_load(g_i[0:1, n:n + 1] if isinstance(n, int) else g_i[0:1, bass.ds(n, 1)],
                                     min_val=0, max_val=E - 1)

            def x_in_tile(n, par, n_half):
                pe.wait_ge(xg_in[par], 16 * (n_half + 1))
                wait(pe, xgt_done, n - 1)
                for c in range(DC):
                    last = nc.tensor.transpose(xt_ps[par][:, c * P:(c + 1) * P],
                                               xg[:, par * D + c * P:par * D + (c + 1) * P], ident[:, :])
                last.then_inc(xgt_ps_done, 1)

            def up(n, par, ex, c):
                pe.wait_ge(xgt_done, n + 1)
                wait(pe, h1_done, 2 * (n - 1) + c + 1)
                for k in range(DC):
                    last = mm(h_ps[c][:, :], xgt[:, (par * DC + k) * P:(par * DC + k + 1) * P],
                              w1_raw[:, bass.ds(ex * (DC * F) + (k * F + c * CH), CH)],
                              start=(k == 0), stop=(k == DC - 1))
                last.then_inc(h_done, 1)

            def hidden_t(n, par):
                for c in range(2):
                    pe.wait_ge(h1_done, 2 * n + c + 1)
                    for k in range(CH // P):
                        col = par * F + c * CH + k * P
                        last = nc.tensor.transpose(ht_ps[c][:, k * P:(k + 1) * P], h1[:, col:col + P], ident[:, :])
                    last.then_inc(ht_done, 1)

            def down(n, par, ex):
                pe.wait_ge(h1t_done, 2 * n + 2)
                for k in range(FC):
                    last = mm(y_ps[par][:, 0:D], h1t[:, par * F + k * P:par * F + (k + 1) * P],
                              w2_raw[:, bass.ds(ex * (FC * D) + k * D, D)], start=(k == 0), stop=(k == FC - 1))
                last.then_inc(y_done, 1)

            pe.wait_ge(plan_done, 1)
            pe.wait_ge(pos_done, 1)
            pe.wait_ge(w1_in, 16)
            x_in_tile(0, 0, 0)
            for c in range(2):
                up(0, 0, expert_of(0), c)
            pe.wait_ge(w2_in, 16)

            def stage(n, par, n_half, last):
                if not last:
                    x_in_tile(n + 1, 1 - par, n_half + par)
                    nxt = expert_of(n + 1)
                    up(n + 1, 1 - par, nxt, 0)
                hidden_t(n, par)
                if not last:
                    up(n + 1, 1 - par, nxt, 1)
                down(n, par, expert_of(n))

            expert_tiles(stage, pe)


def kernel(x, ctx_1024, L0_xattn_ln_gamma, L0_xattn_ln_beta, L0_xattn_w_q, L0_xattn_w_kv, L0_xattn_w_out,
           L0_xattn_b_out, L0_xattn_gate, L0_ffn_Wr, L0_ffn_br, L0_ffn_We1, L0_ffn_be1, L0_ffn_We2, L0_ffn_be2):
    import numpy as np
    import concourse.bacc as bacc
    from concourse.bass_utils import run_bass_kernel_spmd

    ins = {
        "x": x, "ctx": ctx_1024,
        "ln_gamma": np.asarray(L0_xattn_ln_gamma).reshape(DC, P).T, "ln_beta": np.asarray(L0_xattn_ln_beta).reshape(DC, P).T,
        "w_q": L0_xattn_w_q, "w_kv": L0_xattn_w_kv, "w_out": L0_xattn_w_out, "b_out": L0_xattn_b_out,
        "gate": L0_xattn_gate, "w_router_t": np.transpose(np.asarray(L0_ffn_Wr)), "b_router": L0_ffn_br,
        "we1": L0_ffn_We1, "be1": L0_ffn_be1, "we2": L0_ffn_We2, "be2": L0_ffn_be2,
    }
    nc = bacc.Bacc("TRN2", target_bir_lowering=False, num_devices=1)
    arrays, args = {}, []
    for name, a in ins.items():
        a = np.ascontiguousarray(a)
        arrays["in_" + name] = a
        args.append(nc.dram_tensor("in_" + name, a.shape, mybir.dt.from_np(a.dtype), kind="ExternalInput").ap())
    args.append(nc.dram_tensor("out_x", (B, S, D), F32, kind="ExternalOutput").ap())
    attention_and_routed_ffn(nc, *args)
    r = run_bass_kernel_spmd(nc, [arrays], core_ids=[0])
    return r.results[0]["out_x"]
```

```python
import concourse.bass as bass
from concourse import mybir
from contextlib import ExitStack

F32 = mybir.dt.float32
F32R = mybir.dt.float32r
I32 = mybir.dt.int32
U32 = mybir.dt.uint32
ACT = mybir.ActivationFunctionType
ALU = mybir.AluOpType
AX = mybir.AxisListType

B, S, D = 8, 256, 256
H, DH = 16, 64
INNER = H * DH
E, F = 4, 1024
P = 128
EPS = 1e-5
SCALE = DH ** -0.5

HP = H // 2
TB = S // P
NT = B * TB
DC = D // P
FC = F // P
CH = 512
QS = 4
AHEAD = 4
WCH = (3 * D * INNER + INNER * D) // P // CH
CQ, CK, CV, CO = 0, 4, 8, 12
NG = NT + E - 1
RW = D + 3
REG = B * S + P
PAD = S + P
ROWS = E * REG + (E - 1) * P


def attention_and_routed_ffn(nc, x, ctx, gamma, beta, w_q, w_kv, w_out, b_out, gate,
                             w_rt, b_r, we1, be1, we2, be2, out):
    rows_dram = nc.dram_tensor("expert_rows", (ROWS, RW), F32, kind="Internal").ap()
    es = ExitStack()
    with es:
        def sem(name):
            return es.enter_context(nc.semaphore(name))

        def keep(name, shape, dt=F32):
            return es.enter_context(nc.sbuf_tensor(name, shape, dt))

        x_all = keep("x_all", [P, NT * D])
        ident = keep("ident", [P, P])
        gamma_c = keep("gamma_c", [P, DC])
        beta_c = keep("beta_c", [P, DC])
        eps_c = keep("eps_c", [P, TB])
        mhalf_c = keep("mhalf_c", [P, TB])
        gate_c = keep("gate_c", [P, 1])
        tanh_c = keep("tanh_c", [P, 1])
        br_c = keep("br_c", [P, E])
        wr_c = keep("wr_c", [P, DC * E])
        ids = keep("ids", [P, NT], I32)
        run = keep("run", [P, E])
        run_i = keep("run_i", [P, E], I32)
        w1_raw = keep("w1_raw", [P, E * DC * F])

        phase_a = ExitStack()

        def a_sb(name, shape, dt=F32):
            return phase_a.enter_context(nc.sbuf_tensor(name, shape, dt))

        w_hi = a_sb("w_hi", [P, CO * CH], F32R)
        w_lo = a_sb("w_lo", [P, CO * CH], F32R)
        wo_hi = a_sb("wo_hi", [P, (WCH - CO) * CH], F32R)
        wo_lo = a_sb("wo_lo", [P, (WCH - CO) * CH], F32R)
        q_st = a_sb("q_st", [P, QS * 2 * S], F32R)
        k_mv = a_sb("k_mv", [P, QS * 2 * 2 * S], F32R)
        v_sb = a_sb("v_sb", [P, 2 * TB * CH])
        xt_hi = a_sb("xt_hi", [P, 2 * DC * S], F32R)
        xt_lo = a_sb("xt_lo", [P, 2 * DC * S], F32R)
        ct_hi = a_sb("ct_hi", [P, 2 * DC * S], F32R)
        ct_lo = a_sb("ct_lo", [P, 2 * DC * S], F32R)
        c_in = a_sb("c_in", [P, TB * D])
        p_sb = a_sb("p_sb", [P, 4 * TB * S])
        pt_sb = a_sb("pt_sb", [P, 2 * TB * S])
        o_hi = a_sb("o_hi", [P, (HP + 2) * S], F32R)
        o_lo = a_sb("o_lo", [P, (HP + 2) * S], F32R)
        xn = a_sb("xn", [P, TB * D])
        xt_f = a_sb("xt_f", [P, DC * S])
        xf = a_sb("xf", [P, TB * D])
        stage = a_sb("stage", [P, 2 * TB * RW])
        bo_b = a_sb("bo_b", [P, D])
        neg_max = a_sb("neg_max", [P, 4 * TB])
        row_sum = a_sb("row_sum", [P, 4 * TB])
        inv_sum = a_sb("inv_sum", [P, 4 * TB])
        bst = a_sb("bst", [P, TB * 6])
        mv = a_sb("mv", [P, TB * 2])
        rstd = a_sb("rstd", [P, TB])
        var_e = a_sb("var_e", [P, TB])
        bst3 = a_sb("bst3", [P, TB * 6])
        mv3 = a_sb("mv3", [P, TB * 2])
        var_e3 = a_sb("var_e3", [P, TB])
        rstd3 = a_sb("rstd3", [P, TB])
        empty = xn[:, 0:RW]
        lgb = a_sb("lgb", [P, TB * E])
        best = a_sb("best", [P, TB])
        eq = a_sb("eq", [P, TB * E])
        score = a_sb("score", [P, TB * E])
        top = a_sb("top", [P, TB])
        hot = a_sb("hot", [P, TB * E])
        rkc = a_sb("rkc", [P, 2 * TB * E])
        off1 = a_sb("off1", [P, E])
        pos4 = a_sb("pos4", [P, TB * E])
        pos4h = a_sb("pos4h", [P, TB * E])
        pos_f = a_sb("pos_f", [P, TB])
        pos_i = a_sb("pos_i", [P, 2 * TB], I32)
        e_w = a_sb("e_w", [P, E])
        upper = a_sb("upper", [P, P])
        ones_pp = a_sb("ones_pp", [P, P])

        phase_a.close()

        def f_sb(name, shape, dt=F32):
            return keep(name, shape, dt)

        w2_raw = f_sb("w2_raw", [P, E * FC * D])
        b1_b = f_sb("b1_b", [P, E * F])
        b2_b = f_sb("b2_b", [P, E * D])
        ones_e = f_sb("ones_e", [P, E])
        n_f = f_sb("n_f", [P, E])
        n_i = f_sb("n_i", [P, E], I32)
        t_i = f_sb("t_i", [P, E], I32)
        t_f = f_sb("t_f", [P, E])
        t_inc = f_sb("t_inc", [P, E])
        skip = f_sb("skip", [P, E])
        reg0 = f_sb("reg0", [P, E])
        g_io = f_sb("g_io", [P, NG])
        g_ge = f_sb("g_ge", [P, (E - 1) * NG])
        g_sk = f_sb("g_sk", [P, E * NG])
        g_ex = f_sb("g_ex", [P, NG])
        g_row = f_sb("g_row", [P, NG])
        g_i = f_sb("g_i", [P, NG], I32)
        g_r = f_sb("g_r", [P, NG], I32)
        xg = f_sb("xg", [P, 2 * RW])
        xfg = f_sb("xfg", [P, 2 * D])
        xgt = f_sb("xgt", [P, 2 * DC * P])
        h1 = f_sb("h1", [P, 2 * F])
        h1t = f_sb("h1t", [P, 2 * F])
        xb2 = f_sb("xb2", [P, 2 * D])
        idx = f_sb("idx", [P, 2], I32)
        y_sb = f_sb("y_sb", [P, 2 * D])

        banks = [es.enter_context(nc.psum_tensor(f"bank{n}", [P, CH], F32)) for n in range(8)]
        s_ps = banks[0:2]
        t_ps = banks[2:4]
        o_ps = banks[4]
        qk_ps = banks[5:7]
        m_ps = banks[7]
        h_ps = banks[0:2]
        ht_ps = banks[2:4]
        y_ps = banks[4:6]
        xt_ps = banks[6:8]

        x_in, x_rest_in, wq_in, wk_in, wv_in, wo_in, consts_in, gate_in, b1_in = (
            sem(n) for n in ("x_in", "x_rest_in", "wq_in", "wk_in", "wv_in", "wo_in", "consts_in", "gate_in", "b1_in"))
        c_sem = sem("ctx_in")
        w1_in, w2_in = sem("w1_in"), sem("w2_in")
        consts_set, tanh_done, xb_done = sem("consts_set"), sem("tanh_done"), sem("xb_done")
        whi_done, wlo_done = sem("whi_done"), sem("wlo_done")
        qk_done, qk_hi, qk_lo = sem("qk_done"), sem("qk_hi"), sem("qk_lo")
        dup_done = [sem(f"dup_done{n}") for n in range(QS)]
        s_done, mx_done, exp_done, norm_done = sem("s_done"), sem("mx_done"), sem("exp_done"), sem("norm_done")
        inv_done = sem("inv_done")
        t_done, pt_done, pv_done = sem("t_done"), sem("pt_done"), sem("pv_done")
        oh_done, ol_done = sem("oh_done"), sem("ol_done")
        m_done, m_free = sem("m_done"), sem("m_free")
        var_done, rstd_done, xn_done = sem("var_done"), sem("rstd_done"), sem("xn_done")
        xth_done, xt_done = sem("xth_done"), sem("xt_done")
        cth_done, ct_done = sem("cth_done"), sem("ct_done")
        var3_done, rstd3_done = sem("var3_done"), sem("rstd3_done")
        dve_chain = sem("dve_chain")
        dve_passed = sem("dve_passed")
        pool_chain = sem("pool_chain")
        pool_passed = sem("pool_passed")
        phase_a_left, pool_ones = sem("phase_a_left"), sem("pool_ones")
        xf_done, xft_done, hot_done, pos_done = sem("xf_done"), sem("xft_done"), sem("hot_done"), sem("pos_done")
        plan_done, idx_done, xfg_done = sem("plan_done"), sem("idx_done"), sem("xfg_done")
        run_done, padded = sem("run_done"), sem("padded")
        vo_lo_done = sem("vo_lo_done")
        sent = [sem(f"sent{n}") for n in range(2)]
        xg_in = [sem(f"xg_in{n}") for n in range(2)]
        xgt_ps_done, xgt_done = sem("xgt_ps_done"), sem("xgt_done")
        h_done, h1_done, ht_done, h1t_done = sem("h_done"), sem("h1_done"), sem("ht_done"), sem("h1t_done")
        y_done, ysb_done, xb2_done = sem("y_done"), sem("ysb_done"), sem("xb2_done")
        stored = [sem(f"stored{n}") for n in range(2)]

        block = es.enter_context(nc.Block())

        def wait(eng, s, value):
            if not (isinstance(value, int) and value <= 0):
                eng.wait_ge(s, value)

        BEFORE = ("px", "pc", "v0a", "v0b")
        FIRST = ("pc", "px", "v1a", "v1b", "v0a", "v0b")
        JOBS = ("pc", "out0", "out1", "px", "v1a", "tf", "v1b", "lg", "v0a", "rk", "v0b")
        LAST = ("out0", "out1", "v1a", "tf", "v1b", "lg", "rk")
        AFTER = ("out0", "out1", "tf", "lg", "rk")

        def job(b, name):
            if isinstance(b, int):
                lists = [BEFORE, FIRST] + [JOBS] * (B - 2) + [LAST, AFTER]
                return sum(len(l) for l in lists[:b + 1]) + lists[b + 1].index(name)
            return len(BEFORE) + len(FIRST) + len(JOBS) * (b - 1) + JOBS.index(name)

        def wq_ap(w, dc, hp):
            c = (CQ + 2 * dc) * CH + hp * P
            return w[:, c:c + P]

        def wk_ap(w, dc, hp):
            c = (CK + 2 * dc) * CH + hp * P
            return w[:, c:c + P]

        def wv_ap(w, dc, half):
            c = (CV + 2 * dc + half) * CH
            return w[:, c:c + CH]

        def wo_ap(w, hp):
            return w[:, hp * D:(hp + 1) * D]

        SPLIT_FIRST = (CQ, CQ + 2, CK, CK + 2)
        SPLIT_THEN = (CQ + 1, CQ + 3, CK + 1, CK + 3)
        SPLIT = SPLIT_FIRST + SPLIT_THEN + tuple(range(CV, WCH))

        def chunk(w, wo, c):
            return w[:, c * CH:(c + 1) * CH] if c < CO else wo[:, (c - CO) * CH:(c - CO + 1) * CH]

        def stage_ap(p, t, a, z):
            c = (p * TB + t) * RW
            return stage[:, c + a:c + z]

        def stage_col(p, k):
            return stage[:, p * TB * RW:(p + 1) * TB * RW].rearrange("p (t k) -> p t k", t=TB)[:, :, k:k + 1]

        def qst(slot, j):
            return q_st[:, (2 * slot + j) * S:(2 * slot + j + 1) * S]

        def kmv(slot, j, part):
            c = ((2 * slot + j) * 2 + part) * S
            return k_mv[:, c:c + S]

        def o_cols(p, hp):
            c = (hp if hp >= 2 or p == 0 else HP + hp) * S
            return c

        def half(j):
            return slice(DH * j, DH * j + DH)

        def batches(eng_body, eng):
            eng_body(0, 0, 0)
            with eng.Fori(0, (B - 2) // 2) as i:
                eng_body(2 * i + 1, 1, i)
                eng_body(2 * i + 2, 0, i + 1)
            eng_body(B - 1, 1, (B - 1) // 2)

        def is_first(b):
            return isinstance(b, int) and b == 0

        def is_last(b):
            return isinstance(b, int) and b == B - 1

        def expert_tiles(step, eng):
            step(0, 0, 0, False)
            step(1, 1, 0, False)
            with eng.Fori(1, NG // 2 - 1) as i:
                step(2 * i, 0, i, False)
                step(2 * i + 1, 1, i, False)
            assert NG % 2
            for n in range(NG - 3, NG):
                step(n, n % 2, n // 2, n == NG - 1)

        @block.sync
        def _(sp):
            sp.dma_start(x_all[:, 0:TB * D].rearrange("p (t d) -> p t d", d=D),
                         x[0].rearrange("(t p) d -> p t d", p=P)).then_inc(x_in, 16)
            sp.dma_start(c_in[:, :].rearrange("p (t d) -> p t d", d=D),
                         ctx[0].rearrange("(t p) d -> p t d", p=P)).then_inc(c_sem, 16)
            raw = w1_raw
            sp.dma_start(raw[:, CQ * CH:CK * CH].rearrange("p (c n) -> p c n", c=DC),
                         w_q.rearrange("(c p) n -> p c n", p=P)).then_inc(wq_in, 16)
            sp.dma_start(gamma_c[:, :], gamma).then_inc(consts_in, 16)
            sp.dma_start(beta_c[:, :], beta).then_inc(consts_in, 16)
            kv = w_kv.rearrange("(c p) (s n) -> s p c n", p=P, s=2)
            sp.dma_start(raw[:, CK * CH:CV * CH].rearrange("p (c n) -> p c n", c=DC), kv[0]).then_inc(wk_in, 16)
            sp.dma_start(raw[:, CV * CH:CO * CH].rearrange("p (c n) -> p c n", c=DC), kv[1]).then_inc(wv_in, 16)
            sp.dma_start(raw[:, CO * CH:WCH * CH].rearrange("p (c n) -> p c n", c=HP),
                         w_out.rearrange("(c p) n -> p c n", p=P)).then_inc(wo_in, 16)
            sp.dma_start(gate_c[:, :], gate.partition_broadcast(P)).then_inc(gate_in, 16)
            sp.dma_start(bo_b[:, :], b_out.partition_broadcast(P)).then_inc(gate_in, 16)
            sp.dma_start(br_c[:, :], b_r.partition_broadcast(P)).then_inc(gate_in, 16)
            sp.dma_start(wr_c[:, :].rearrange("p (c e) -> p c e", c=DC),
                         w_rt.rearrange("(c p) e -> p c e", p=P)).then_inc(gate_in, 16)
            sp.dma_start(x_all[:, TB * D:].rearrange("p (t d) -> p t d", d=D),
                         x[1:].rearrange("b (t p) d -> p (b t) d", p=P)).then_inc(x_rest_in, 16)
            sp.wait_ge(m_done, job(-1, "pc") + 1)
            sp.dma_start(c_in[:, :].rearrange("p (t d) -> p t d", d=D),
                         ctx[1].rearrange("(t p) d -> p t d", p=P)).then_inc(c_sem, 16)

            def dup(u, slot):
                sp.wait_ge(qk_lo, u + 1)
                for j in range(2):
                    c = (2 * slot + j) * 2 * S
                    sp.dma_start(k_mv[half(1 - j), c:c + 2 * S].bitcast(F32),
                                 k_mv[half(j), c:c + 2 * S].bitcast(F32)).then_inc(dup_done[slot], 16)

            dup(0, 0)
            dup(1, 1)
            dup(2, 2)

            def body(b, p, b_half):
                u0 = 8 * b
                for hp in range(HP):
                    if not is_last(b) or hp + 3 < HP:
                        dup(u0 + hp + 3, (hp + 3) % QS)
                    if hp == 1 and not (isinstance(b, int) and b >= B - 2):
                        sp.wait_ge(m_done, job(b, "pc") + 1)
                        nb = b + 2
                        src = ctx[nb] if isinstance(b, int) else ctx[bass.ds(nb, 1)].rearrange("o r d -> (o r) d")
                        sp.dma_start(c_in[:, :].rearrange("p (t d) -> p t d", d=D),
                                     src.rearrange("(t p) d -> p t d", p=P)).then_inc(c_sem, 16)

            body(0, 0, 0)
            with sp.Fori(0, (B - 2) // 2 - 1) as i:
                body(2 * i + 1, 1, i)
                body(2 * i + 2, 0, i + 1)
            for b in range(B - 3, B):
                body(b, b % 2, b // 2)

            def pad(first_row, rows):
                sp.dma_start(rows_dram[first_row, :].rearrange("(g p) d -> p g d", p=P),
                             empty[:, :].unsqueeze(1).broadcast_to((P, rows // P, RW))).then_inc(padded, 16)

            sp.wait_ge(pool_ones, 1)
            pad(slice(E * REG, ROWS), (E - 1) * P)
            sp.wait_ge(run_done, 1)
            for e in range(E):
                row = sp.value_load(run_i[0:1, e:e + 1], min_val=0, max_val=ROWS - PAD)
                pad(bass.ds(row, PAD), PAD)

            sp.wait_ge(phase_a_left, 1)
            sp.dma_start(b2_b[:, :], be2.rearrange("e n -> (e n)").partition_broadcast(P)).then_inc(b1_in, 16)

            def load_rows(n, par):
                row = sp.value_load(g_r[0:1, n:n + 1] if isinstance(n, int) else g_r[0:1, bass.ds(n, 1)],
                                    min_val=0, max_val=ROWS - P)
                sp.dma_start(xg[:, par * RW:(par + 1) * RW], rows_dram[bass.ds(row, P), :]).then_inc(xg_in[par], 16)

            sp.wait_ge(plan_done, 1)
            for n in range(2):
                sp.wait_ge(sent[n], 32 * (B // 2))
            load_rows(0, 0)
            load_rows(1, 1)
            with sp.Fori(0, NG // 2 - 1) as i:
                for par in range(2):
                    n = 2 * i + par
                    sp.wait_ge(xfg_done, n + 1)
                    sp.wait_ge(idx_done, n + 1)
                    load_rows(n + 2, par)
            sp.wait_ge(xfg_done, NG - 2)
            sp.wait_ge(idx_done, NG - 2)
            load_rows(NG - 1, 0)
            for n in range(2):
                sp.wait_ge(stored[n], 16 * ((NG + 1 - n) // 2))

        @block.gpsimd
        def _(pool):
            g = nc.gpsimd
            count = [0]

            def link(ins):
                count[0] += 1
                ins.then_inc(pool_chain, 1)
                pool.wait_ge(pool_chain, count[0])

            g.iota(ids[:, :], [[P, NT]], base=0, channel_multiplier=1)
            g.memset(eps_c[:, :], EPS)
            g.memset(mhalf_c[:, :], -0.5)
            link(g.memset(ident[:, :], 0.0))
            g.affine_select(out=ident[:, :], in_=ident[:, :], compare_op=ALU.not_equal, fill=1.0, base=0,
                            pattern=[[-1, P]], channel_multiplier=1).then_inc(consts_set, 1)
            g.iota(e_w[:, :], [[-1, E]], base=E, channel_multiplier=0, allow_small_or_imprecise_dtypes=True)
            g.iota(run[:, :], [[REG, E]], base=0, channel_multiplier=0, allow_small_or_imprecise_dtypes=True)
            link(g.memset(ones_pp[:, :], 1.0))
            g.affine_select(out=upper[:, :], in_=ones_pp[:, :], compare_op=ALU.is_gt, fill=0.0, base=0,
                            pattern=[[1, P]], channel_multiplier=-1).then_inc(consts_set, 1)

            def make_empty_row():
                pool.wait_ge(m_done, job(B - 2, "px") + 1)
                link2(g.memset(empty[:, :], 0.0))
                g.iota(empty[:, RW - 1:RW].bitcast(I32), [[0, 1]], base=B * S,
                       channel_multiplier=1).then_inc(pool_ones, 1)

            def send(b, p, b_half):
                wait(pool, pos_done, b + 1)
                pool.sem_inc(pool_passed, 1)
                for t in range(TB):
                    g.indirect_dma_start(out=rows_dram[:, :],
                                         out_offset=bass.IndirectOffsetOnAxis(
                                             ap=pos_i[:, p * TB + t:p * TB + t + 1].bitcast(U32), axis=0),
                                         in_=stage_ap(p, t, 0, RW), in_offset=None).then_inc(sent[p], 16)

            def rstd_step(src, tmp, dst, ready, value, done):
                wait(pool, ready, value)
                link2(g.tensor_tensor(tmp[:, :], src[:, 1:2 * TB:2], eps_c[:, :], ALU.add))
                g.tensor_tensor(dst[:, :], tmp[:, :], mhalf_c[:, :], ALU.pow).then_inc(done, 1)

            def add_b_out(b):
                pool.wait_ge(xn_done, b + 1)
                n = TB * D
                xb = x_all[:, b * n:b * n + n] if isinstance(b, int) else x_all[:, bass.ds(b * n, n)]
                xb = xb.rearrange("p (t d) -> p t d", t=TB)
                g.tensor_tensor(xb, xb, bo_b[:, :].unsqueeze(1).broadcast_to((P, TB, D)), ALU.add).then_inc(xb_done, 1)

            def b_out_gated():
                pool.wait_ge(tanh_done, 1)
                pool.wait_ge(gate_in, 64)
                link2(g.tensor_scalar(bo_b[:, :], bo_b[:, :], tanh_c[:, 0:1], None, ALU.mult))

            def normalise(u, par, j):
                pool.wait_ge(inv_done, 2 * u + j + 1)
                slot = 2 * par + j
                pv = p_sb[:, slot * TB * S:(slot + 1) * TB * S].rearrange("p (t k) -> p t k", t=TB)
                rs = inv_sum[:, slot * TB:(slot + 1) * TB].unsqueeze(2).broadcast_to((P, TB, S))
                g.tensor_tensor(pv, pv, rs, ALU.mult).then_inc(norm_done, 1)

            chain = {"base": count[0], "n": 0}
            PER_BATCH = 3

            def link2(ins):
                chain["n"] += 1
                ins.then_inc(pool_chain, 1)
                pool.wait_ge(pool_chain, chain["base"] + chain["n"])

            pool.wait_ge(consts_set, 1)
            rstd_step(mv, var_e, rstd, var_done, 1, rstd_done)
            rstd_step(mv, var_e, rstd, var_done, 2, rstd_done)
            def split_lo(c):
                pool.wait_ge(whi_done, SPLIT.index(c) + 1)
                g.tensor_tensor(chunk(w_lo, wo_lo, c), w1_raw[:, c * CH:(c + 1) * CH],
                                chunk(w_hi, wo_hi, c).bitcast(F32), ALU.subtract).then_inc(vo_lo_done, 1)

            for c in range(CV, CO):
                split_lo(c)
            b_out_gated()
            base0 = chain["base"] + chain["n"]

            for j in range(2):
                normalise(0, 0, j)

            def body(b, p, b_half):
                first, last = is_first(b), is_last(b)
                chain["base"], chain["n"] = base0 if first else base0 + 2 + PER_BATCH * (b - 1), 0
                u0 = 8 * b
                for hp in range(HP):
                    if not (last and hp == HP - 1):
                        for j in range(2):
                            normalise(u0 + hp + 1, (hp + 1) % 2, j)
                    if hp in (0, 1) and not last:
                        rstd_step(mv, var_e, rstd, var_done, 2 * b + 3 + hp, rstd_done)
                    if hp == 2 and not first:
                        rstd_step(mv3, var_e3, rstd3, var3_done, b, rstd3_done)
                    if hp == 5:
                        add_b_out(b)
                    if last and hp == 0:
                        make_empty_row()
                    if first and hp < WCH - CO:
                        split_lo(CO + hp)
                    if hp == 7 and not (first or last):
                        send(b - 1, 1 - p, b_half)

            batches(body, pool)
            chain["base"], chain["n"] = base0 + 2 + PER_BATCH * (B - 2) + 2, 0
            rstd_step(mv3, var_e3, rstd3, var3_done, B, rstd3_done)

            pool.wait_ge(phase_a_left, 1)
            g.memset(ones_e[:, :], 1.0)
            g.iota(g_io[:, :], [[1, NG]], base=0, channel_multiplier=0, allow_small_or_imprecise_dtypes=True)
            g.iota(reg0[:, :], [[REG, E]], base=0, channel_multiplier=0,
                   allow_small_or_imprecise_dtypes=True).then_inc(consts_set, 1)
            send(B - 2, 0, 0)
            pool.wait_ge(padded, 16 * (E + 1))
            send(B - 1, 1, 0)

            def expert_of(n):
                return pool.value_load(g_i[0:1, n:n + 1] if isinstance(n, int) else g_i[0:1, bass.ds(n, 1)],
                                       min_val=0, max_val=E - 1)

            def tile_x(n, par, n_half, ex):
                pool.wait_ge(xg_in[par], 16 * (n_half + 1))
                wait(pool, ysb_done, n - 1)
                g.tensor_tensor(xb2[:, par * D:(par + 1) * D], xg[:, par * RW:par * RW + D],
                                b2_b[:, bass.ds(ex * D, D)], ALU.add).then_inc(xb2_done, 1)
                wait(pool, stored[par], 16 * n_half)
                pool.sem_inc(pool_passed, 1)
                g.tensor_copy(idx[:, par:par + 1],
                              xg[:, (par + 1) * RW - 1:(par + 1) * RW].bitcast(I32)).then_inc(idx_done, 1)

            pool.wait_ge(plan_done, 1)
            pool.wait_ge(b1_in, 32)
            tile_x(0, 0, 0, expert_of(0))

            def step(n, par, n_half, last):
                if not last:
                    tile_x(n + 1, 1 - par, n_half + par, expert_of(n + 1))
                pool.wait_ge(ysb_done, n + 1)
                pool.wait_ge(idx_done, n + 1)
                pool.sem_inc(pool_passed, 1)
                g.indirect_dma_start(out=out.rearrange("b s d -> (b s) d"),
                                     out_offset=bass.IndirectOffsetOnAxis(ap=idx[:, par:par + 1].bitcast(U32), axis=0),
                                     in_=y_sb[:, par * D:(par + 1) * D], in_offset=None,
                                     bounds_check=B * S - 1, oob_is_err=False).then_inc(stored[par], 16)

            expert_tiles(step, pool)

        @block.scalar
        def _(act):
            a = nc.scalar

            def split_hi(c, arrived):
                if arrived is not None:
                    act.wait_ge(arrived, 16)
                a.activation(chunk(w_hi, wo_hi, c), w1_raw[:, c * CH:(c + 1) * CH], ACT.Copy).then_inc(whi_done, 1)

            def ctx_hi(b, jb, par):
                act.wait_ge(m_done, jb + 1)
                a.activation(ct_hi[:, par * DC * S:(par + 1) * DC * S], m_ps[:, :],
                             ACT.Copy).then_inc(cth_done, 1)

            def x_hi(jb, par):
                act.wait_ge(m_free, jb + 1)
                a.activation(xt_hi[:, par * DC * S:(par + 1) * DC * S], xt_f[:, :], ACT.Copy).then_inc(xth_done, 1)

            def qk_high(u, slot):
                act.wait_ge(qk_done, u + 1)
                for j in range(2):
                    a.activation(qst(slot, j)[half(j), :], qk_ps[slot % 2][half(j), 0:S], ACT.Copy, scale=SCALE)
                for j in range(2):
                    last = a.activation(kmv(slot, j, 0)[half(j), :], qk_ps[slot % 2][half(j), S:2 * S], ACT.Copy)
                last.then_inc(qk_hi, 1)

            def exponentials(u, par, j):
                act.wait_ge(mx_done, 2 * u + j + 1)
                wait(act, t_done, 2 * (u - 2) + j + 1)
                slot = 2 * par + j
                for t in range(TB):
                    last = a.activation(p_sb[:, (slot * TB + t) * S:(slot * TB + t + 1) * S],
                                        s_ps[j][:, t * S:(t + 1) * S], ACT.Exp,
                                        bias=neg_max[:, slot * TB + t:slot * TB + t + 1],
                                        accum_out=row_sum[:, slot * TB + t:slot * TB + t + 1])
                last.then_inc(exp_done, 1)

            def evacuate_pt(u, j):
                act.wait_ge(t_done, 2 * u + j + 1)
                a.activation(pt_sb[:, j * TB * S:(j + 1) * TB * S], t_ps[j][:, :], ACT.Copy).then_inc(pt_done, 1)

            def out_high(u, p, hp):
                act.wait_ge(pv_done, u + 1)
                c = o_cols(p, hp)
                a.activation(o_hi[:, c:c + S], o_ps[:, 0:S], ACT.Copy).then_inc(oh_done, 1)

            for c in SPLIT_FIRST:
                split_hi(c, {CQ: wq_in, CK: wk_in}.get(c))
            x_hi(job(-1, "px"), 0)
            ctx_hi(0, job(-1, "pc"), 0)
            for c in SPLIT_THEN:
                split_hi(c, None)
            for c in range(CV, CO):
                split_hi(c, {CV: wv_in}.get(c))
            qk_high(0, 0)
            qk_high(1, 1)
            qk_high(2, 2)
            act.wait_ge(gate_in, 64)
            a.activation(tanh_c[:, :], gate_c[:, :], ACT.Tanh).then_inc(tanh_done, 1)
            exponentials(0, 0, 0)
            exponentials(0, 0, 1)
            def body(b, p, b_half):
                u0 = 8 * b
                last = is_last(b)
                for hp in range(HP):
                    u = u0 + hp
                    if not (is_first(b) and hp < 2):
                        out_high(u - 2, p if hp >= 2 else 1 - p, (hp - 2) % HP)
                    if not (is_first(b) and hp == 0):
                        evacuate_pt(u - 1, 0)
                        evacuate_pt(u - 1, 1)
                    if not last or hp + 3 < HP:
                        qk_high(u + 3, (hp + 3) % QS)
                    if hp == 0 and not last:
                        ctx_hi(b + 1, job(b, "pc"), 1 - p)
                    if not (last and hp == HP - 1):
                        exponentials(u + 1, (hp + 1) % 2, 0)
                        exponentials(u + 1, (hp + 1) % 2, 1)
                    if hp == 3 and not last:
                        x_hi(job(b, "px"), 1 - p)
                    if is_first(b) and hp < WCH - CO:
                        split_hi(CO + hp, wo_in)
                    if is_first(b) and hp >= WCH - CO:
                        e = hp - (WCH - CO)
                        act.wait_ge(wlo_done, CV)
                        act.wait_ge(vo_lo_done, WCH - CV)
                        act.dma_start(w1_raw[:, e * DC * F:(e + 1) * DC * F].rearrange("p (c n) -> p c n", n=F),
                                      we1[e].rearrange("(c p) n -> p c n", p=P)).then_inc(w1_in, 16)
                    if last and hp == 5:
                        act.wait_ge(m_done, job(b, "v1b") + 1)
                        act.dma_start(w2_raw[:, :].rearrange("p (ec n) -> p ec n", n=D),
                                      we2.rearrange("e (c p) n -> p (e c) n", p=P)).then_inc(w2_in, 16)
                        act.dma_start(b1_b[:, :],
                                      be1.rearrange("e n -> (e n)").partition_broadcast(P)).then_inc(b1_in, 16)

            batches(body, act)
            out_high(B * HP - 2, 1, HP - 2)
            evacuate_pt(B * HP - 1, 0)
            evacuate_pt(B * HP - 1, 1)
            out_high(B * HP - 1, 1, HP - 1)

            def xg_evacuate(n, par):
                act.wait_ge(xgt_ps_done, n + 1)
                a.activation(xgt[:, par * DC * P:(par + 1) * DC * P], xt_ps[par][:, 0:DC * P],
                             ACT.Copy).then_inc(xgt_done, 1)

            act.wait_ge(phase_a_left, 1)
            xg_evacuate(0, 0)
            xg_evacuate(1, 1)

            def step(n, par, n_half, last):
                for c in range(2):
                    act.wait_ge(ht_done, 2 * n + c + 1)
                    a.activation(h1t[:, par * F + c * CH:par * F + (c + 1) * CH], ht_ps[c][:, :],
                                 ACT.Relu).then_inc(h1t_done, 1)
                if not (last or isinstance(n, int) and n + 2 >= NG):
                    xg_evacuate(n + 2, par)

            expert_tiles(step, act)

        @block.vector
        def _(dve):
            v = nc.vector
            chain = {"base": 0, "n": 0}

            def link(ins):
                chain["n"] += 1
                ins.then_inc(dve_chain, 1)
                dve.wait_ge(dve_chain, chain["base"] + chain["n"])

            def x_tile(b, t):
                if isinstance(b, int):
                    c = (TB * b + t) * D
                    return x_all[:, c:c + D]
                return x_all[:, bass.ds((b * TB + t) * D, D)]

            def moments(src, st, dst, done):
                for t in range(TB):
                    last = v.bn_stats(st[:, 6 * t:6 * t + 6], src(t))
                link(last)
                dve.sem_inc(dve_passed, 1)
                for t in range(TB):
                    last = v.bn_aggr(dst[:, 2 * t:2 * t + 2], st[:, 6 * t:6 * t + 6])
                last.then_inc(done, 1)

            def standardise(dst, src, m, r):
                for t in range(TB):
                    last = v.tensor_scalar(dst[:, t * D:(t + 1) * D], src(t), m[:, 2 * t:2 * t + 1],
                                           r[:, t:t + 1], ALU.subtract, ALU.mult)
                return last

            def xn_tile(t):
                return xn[:, t * D:(t + 1) * D]

            def split_lo(c):
                dve.wait_ge(whi_done, SPLIT.index(c) + 1)
                v.tensor_tensor(chunk(w_lo, wo_lo, c), w1_raw[:, c * CH:(c + 1) * CH],
                                chunk(w_hi, wo_hi, c).bitcast(F32), ALU.subtract).then_inc(wlo_done, 1)

            def norm_a(b):
                moments(lambda t: x_tile(b, t), bst, mv, var_done)

            def norm_b(b):
                dve.wait_ge(rstd_done, 2 * b + 1)
                link(standardise(xn, lambda t: x_tile(b, t), mv, rstd))
                moments(xn_tile, bst, mv, var_done)

            def norm_c(b):
                dve.wait_ge(rstd_done, 2 * b + 2)
                standardise(xn, xn_tile, mv, rstd).then_inc(xn_done, 1)

            def x_affine(b, jb):
                dve.wait_ge(m_done, jb + 1)
                for c in range(DC):
                    last = v.tensor_scalar(xt_f[:, c * S:(c + 1) * S], m_ps[:, c * S:(c + 1) * S],
                                           gamma_c[:, c:c + 1], beta_c[:, c:c + 1], ALU.mult, ALU.add)
                last.then_inc(m_free, 1)

            def x_low(b, par):
                dve.wait_ge(xth_done, b + 1)
                s = slice(par * DC * S, (par + 1) * DC * S)
                v.tensor_tensor(xt_lo[:, s], xt_f[:, :], xt_hi[:, s].bitcast(F32), ALU.subtract).then_inc(xt_done, 1)

            def ctx_low(b, par):
                dve.wait_ge(cth_done, b + 1)
                s = slice(par * DC * S, (par + 1) * DC * S)
                v.tensor_tensor(ct_lo[:, s], m_ps[:, :], ct_hi[:, s].bitcast(F32),
                                ALU.subtract).then_inc(m_free, 1)

            def v_evacuate(jb, hf, kt):
                dve.wait_ge(m_done, jb + 1)
                c = (hf * TB + kt) * CH
                v.tensor_copy(v_sb[:, c:c + CH], m_ps[:, :]).then_inc(m_free, 1)

            def residual(b, p, b_half, t, jb):
                dve.wait_ge(m_done, jb + 1)
                if t == 0:
                    dve.wait_ge(xb_done, b + 1)
                    wait(dve, sent[p], 32 * b_half)
                v.scalar_tensor_tensor(out=stage_ap(p, t, 0, D), in0=m_ps[:, 0:D], scalar=tanh_c[:, 0:1],
                                       in1=x_tile(b, t), op0=ALU.mult, op1=ALU.add).then_inc(m_free, 1)

            def qk_low(u, slot):
                dve.wait_ge(qk_hi, u + 1)
                for j in range(2):
                    v.scalar_tensor_tensor(out=qst(slot, j)[half(1 - j), :], in0=qk_ps[slot % 2][half(j), 0:S], scalar=SCALE,
                                           in1=qst(slot, j)[half(j), :].bitcast(F32), op0=ALU.mult, op1=ALU.subtract)
                for j in range(2):
                    last = v.tensor_tensor(kmv(slot, j, 1)[half(j), :], qk_ps[slot % 2][half(j), S:2 * S],
                                           kmv(slot, j, 0)[half(j), :].bitcast(F32), ALU.subtract)
                last.then_inc(qk_lo, 1)

            def maxima(u, par, j):
                dve.wait_ge(s_done, 2 * u + j + 1)
                slot = 2 * par + j
                v.tensor_reduce(neg_max[:, slot * TB:(slot + 1) * TB],
                                s_ps[j][:, :].rearrange("p (t k) -> p t k", t=TB), AX.X, ALU.max,
                                negate=True).then_inc(mx_done, 1)

            def inverse_sums(u, par, j):
                dve.wait_ge(exp_done, 2 * u + j + 1)
                slot = 2 * par + j
                v.reciprocal(inv_sum[:, slot * TB:(slot + 1) * TB],
                             row_sum[:, slot * TB:(slot + 1) * TB]).then_inc(inv_done, 1)

            def out_low(u, p, hp):
                dve.wait_ge(oh_done, u + 1)
                s = slice(o_cols(p, hp), o_cols(p, hp) + S)
                v.tensor_tensor(o_lo[:, s], o_ps[:, 0:S], o_hi[:, s].bitcast(F32), ALU.subtract).then_inc(ol_done, 1)

            def rows(p):
                return lambda t: stage_ap(p, t, 0, D)

            def ffn_norm_a(b, p, jb):
                dve.wait_ge(m_free, jb + 1)
                moments(rows(p), bst3, mv3, var3_done)

            def ffn_norm_b(b, p):
                dve.wait_ge(rstd3_done, b + 1)
                standardise(xf, rows(p), mv3, rstd3).then_inc(xf_done, 1)
                v.tensor_copy(stage_col(p, D), mv3[:, 0::2].unsqueeze(2))
                v.tensor_copy(stage_col(p, D + 1), rstd3[:, :].unsqueeze(2))
                src = ids[:, TB * b:TB * b + TB] if isinstance(b, int) else ids[:, bass.ds(b * TB, TB)]
                v.tensor_copy(stage_col(p, D + 2).bitcast(I32), src.unsqueeze(2))

            by_expert = lambda tl: tl[:, :].rearrange("p (t e) -> p t e", e=E)

            def xf_evacuate(jb, split):
                dve.wait_ge(xt_done, split)
                dve.wait_ge(m_done, jb + 1)
                v.tensor_copy(xt_f[:, :], m_ps[:, :]).then_inc(m_free, 1)

            def logits(jb):
                dve.wait_ge(m_done, jb + 1)
                v.tensor_tensor(by_expert(lgb), m_ps[:, 0:TB * E].rearrange("p (t e) -> p t e", e=E),
                                br_c[:, :].unsqueeze(1).broadcast_to((P, TB, E)), ALU.add).then_inc(m_free, 1)

            def choose(jb):
                dve.wait_ge(m_free, jb + 1)
                link(v.tensor_reduce(best[:, :], by_expert(lgb), AX.X, ALU.max))
                link(v.tensor_tensor(by_expert(eq), by_expert(lgb),
                                     best[:, :].unsqueeze(2).broadcast_to((P, TB, E)), ALU.is_ge))
                weights = e_w[:, :].unsqueeze(1).broadcast_to((P, TB, E))
                link(v.tensor_tensor(by_expert(score), by_expert(eq), weights, ALU.mult))
                link(v.tensor_reduce(top[:, :], by_expert(score), AX.X, ALU.max))
                v.tensor_tensor(by_expert(hot), weights, top[:, :].unsqueeze(2).broadcast_to((P, TB, E)),
                                ALU.is_equal).then_inc(hot_done, 1)

            def ranks(jb):
                dve.wait_ge(m_done, jb + 1)
                v.tensor_copy(rkc[:, :], m_ps[:, 0:2 * TB * E]).then_inc(m_free, 1)

            def places(jb, p):
                dve.wait_ge(m_free, jb + 1)
                rank = lambda t: rkc[:, t * E:(t + 1) * E]
                count = lambda t: rkc[:, (TB + t) * E:(TB + t + 1) * E]
                v.tensor_tensor(pos4[:, 0:E], rank(0), run[:, :], ALU.add)
                link(v.tensor_tensor(off1[:, :], run[:, :], count(0), ALU.add))
                v.tensor_tensor(pos4[:, E:2 * E], rank(1), off1[:, :], ALU.add)
                link(v.tensor_tensor(run[:, :], off1[:, :], count(1), ALU.add))
                link(v.tensor_tensor(pos4h[:, :], pos4[:, :], hot[:, :], ALU.mult))
                link(v.tensor_reduce(pos_f[:, :], by_expert(pos4h), AX.X, ALU.add))
                v.tensor_copy(pos_i[:, p * TB:(p + 1) * TB], pos_f[:, :]).then_inc(pos_done, 1)

            dve.wait_ge(x_in, 16)
            norm_a(0)
            norm_b(0)
            norm_c(0)
            dve.wait_ge(consts_in, 32)
            x_affine(0, job(-1, "px"))
            for c in SPLIT_FIRST:
                split_lo(c)
            x_low(0, 0)
            ctx_low(0, 0)
            for c in SPLIT_THEN:
                split_lo(c)
            qk_low(0, 0)
            qk_low(1, 1)
            qk_low(2, 2)
            v_evacuate(job(-1, "v0a"), 0, 0)
            v_evacuate(job(-1, "v0b"), 0, 1)
            dve.wait_ge(gate_in, 64)
            dve.wait_ge(consts_set, 2)
            dve.wait_ge(x_rest_in, 16)
            maxima(0, 0, 0)
            maxima(0, 0, 1)
            inverse_sums(0, 0, 0)
            inverse_sums(0, 0, 1)
            base0 = chain["base"] + chain["n"]
            PER_BATCH = 3 + 1 + 4 + 4

            def body(b, p, b_half):
                first, last = is_first(b), is_last(b)
                chain["base"], chain["n"] = base0 if first else base0 + 3 + PER_BATCH * (b - 1), 0
                u0 = 8 * b
                for hp in range(HP):
                    u = u0 + hp
                    if hp == 3 and not last:
                        x_affine(b + 1, job(b, "px"))
                    if hp == 4:
                        if not last:
                            x_low(b + 1, 1 - p)
                        if not first:
                            xf_evacuate(job(b, "tf"), B if last else b + 2)
                    if hp == 5 and not first:
                        logits(job(b, "lg"))
                    if hp == 6 and not first:
                        ranks(job(b, "rk"))
                    if not (first and hp < 2):
                        out_low(u - 2, p if hp >= 2 else 1 - p, (hp - 2) % HP)
                    if not (last and hp == HP - 1):
                        maxima(u + 1, (hp + 1) % 2, 0)
                        maxima(u + 1, (hp + 1) % 2, 1)
                    if not last or hp + 3 < HP:
                        qk_low(u + 3, (hp + 3) % QS)
                    if not (last and hp == HP - 1):
                        inverse_sums(u + 1, (hp + 1) % 2, 0)
                        inverse_sums(u + 1, (hp + 1) % 2, 1)
                    if hp in (1, 2) and not first:
                        residual(b - 1, 1 - p, b_half if p else b_half - 1, hp - 1, job(b, f"out{hp - 1}"))
                    if not last:
                        if hp == 0:
                            ctx_low(b + 1, 1 - p)
                            norm_a(b + 1)
                        if hp == 1:
                            norm_b(b + 1)
                        if hp == 2:
                            norm_c(b + 1)
                    if hp in (3, 4):
                        v_evacuate(job(b, f"v1{'ab'[hp - 3]}"), 1, hp - 3)
                    if hp in (5, 6) and not last:
                        v_evacuate(job(b, f"v0{'ab'[hp - 5]}"), 0, hp - 5)
                    if not first:
                        if hp == 2:
                            ffn_norm_a(b - 1, 1 - p, job(b, "out1"))
                        if hp == 3:
                            ffn_norm_b(b - 1, 1 - p)
                        if hp == 5:
                            choose(job(b, "lg"))
                        if hp == 6:
                            places(job(b, "rk"), 1 - p)
                        if last and hp == 6:
                            v.tensor_copy(run_i[:, :], run[:, :]).then_inc(run_done, 1)
                assert chain["n"] == (3 if first else PER_BATCH - 3 if last else PER_BATCH)

            batches(body, dve)
            chain["base"], chain["n"] = base0 + 3 + PER_BATCH * (B - 2) + PER_BATCH - 3, 0
            out_low(B * HP - 2, 1, HP - 2)
            out_low(B * HP - 1, 1, HP - 1)
            for t in range(TB):
                residual(B - 1, 1, (B - 1) // 2, t, job(B, f"out{t}"))
            v.memset(b2_b[:, 0:1], 0.0).then_inc(phase_a_left, 1)
            ffn_norm_a(B - 1, 1, job(B, "out1"))
            ffn_norm_b(B - 1, 1)
            xf_evacuate(job(B, "tf"), B)
            logits(job(B, "lg"))
            choose(job(B, "lg"))
            ranks(job(B, "rk"))
            places(job(B, "rk"), 1)

            dve.wait_ge(consts_set, 3)
            link(v.tensor_tensor(n_f[:, :], run[:, :], reg0[:, :], ALU.subtract))
            link(v.tensor_scalar(n_f[:, :], n_f[:, :], float(P - 1), None, ALU.add))
            link(v.tensor_copy(n_i[:, :], n_f[:, :]))
            link(v.tensor_scalar(t_i[:, :], n_i[:, :], P.bit_length() - 1, None, ALU.arith_shift_right))
            link(v.tensor_copy(t_f[:, :], t_i[:, :]))
            v.tensor_scalar(skip[:, :], t_f[:, :], -float(P), float(REG), ALU.mult, ALU.add)
            link(v.tensor_tensor_scan(t_inc[:, :], ones_e[:, :], t_f[:, :], 0.0, ALU.mult, ALU.add))
            for e in range(E):
                s = slice(e * NG, (e + 1) * NG)
                if e < E - 1:
                    v.tensor_scalar(g_ge[:, s], g_io[:, :], t_inc[:, e:e + 1], None, ALU.is_ge)
                last = v.tensor_scalar(g_sk[:, s], g_io[:, :], t_inc[:, e:e + 1], skip[:, e:e + 1], ALU.is_ge, ALU.mult)
            link(last)
            v.tensor_tensor(g_ex[:, :], g_ge[:, 0:NG], g_ge[:, NG:2 * NG], ALU.add)
            v.scalar_tensor_tensor(out=g_row[:, :], in0=g_io[:, :], scalar=float(P), in1=g_sk[:, 0:NG],
                                   op0=ALU.mult, op1=ALU.add).then_inc(dve_chain, 1)
            chain["n"] += 1
            dve.wait_ge(dve_chain, chain["base"] + chain["n"])
            v.tensor_tensor(g_ex[:, :], g_ex[:, :], g_ge[:, 2 * NG:3 * NG], ALU.add)
            link(v.tensor_tensor(g_row[:, :], g_row[:, :], g_sk[:, NG:2 * NG], ALU.add))
            v.tensor_copy(g_i[:, :], g_ex[:, :])
            link(v.tensor_tensor(g_row[:, :], g_row[:, :], g_sk[:, 2 * NG:3 * NG], ALU.add))
            link(v.tensor_tensor(g_row[:, :], g_row[:, :], g_sk[:, 3 * NG:4 * NG], ALU.add))
            v.tensor_copy(g_r[:, :], g_row[:, :]).then_inc(plan_done, 1)

            dve.wait_ge(b1_in, 32)
            dve.wait_ge(plan_done, 1)

            def expert_of(n):
                return dve.value_load(g_i[0:1, n:n + 1] if isinstance(n, int) else g_i[0:1, bass.ds(n, 1)],
                                      min_val=0, max_val=E - 1)

            def h_bias(n, par, ex):
                for c in range(2):
                    dve.wait_ge(h_done, 2 * n + c + 1)
                    col = par * F + c * CH
                    v.tensor_tensor(h1[:, col:col + CH], h_ps[c][:, :],
                                    b1_b[:, bass.ds(ex * F + c * CH, CH)], ALU.add).then_inc(h1_done, 1)

            def tile_norm(n, par, n_half):
                dve.wait_ge(xg_in[par], 16 * (n_half + 1))
                wait(dve, xgt_ps_done, n - 1)
                c = par * RW
                v.tensor_scalar(xfg[:, par * D:(par + 1) * D], xg[:, c:c + D], xg[:, c + D:c + D + 1],
                                xg[:, c + D + 1:c + D + 2], ALU.subtract, ALU.mult).then_inc(xfg_done, 1)

            def y_add(n, par, n_half):
                dve.wait_ge(y_done, n + 1)
                dve.wait_ge(xb2_done, n + 1)
                wait(dve, stored[par], 16 * n_half)
                v.tensor_tensor(y_sb[:, par * D:(par + 1) * D], y_ps[par][:, 0:D],
                                xb2[:, par * D:(par + 1) * D], ALU.add).then_inc(ysb_done, 1)

            tile_norm(0, 0, 0)
            tile_norm(1, 1, 0)
            h_bias(0, 0, expert_of(0))

            def step(n, par, n_half, last):
                if not (last or isinstance(n, int) and n + 2 >= NG):
                    tile_norm(n + 2, par, n_half + 1)
                if not last:
                    h_bias(n + 1, 1 - par, expert_of(n + 1))
                y_add(n, par, n_half)

            expert_tiles(step, dve)

        @block.tensor
        def _(pe):
            mm = nc.tensor.matmul

            def three(outp, terms):
                n = len(terms)
                for k, (lh, ll, rh, rl) in enumerate(terms):
                    mm(outp, lh, rh, start=(k == 0), stop=False)
                    mm(outp, lh, rl, start=False, stop=False)
                    last = mm(outp, ll, rh, start=False, stop=(k == n - 1))
                return last

            def project_qk(u, hp, par):
                wait(pe, qk_lo, u - 1)
                bank = qk_ps[hp % 2]
                s = [slice((par * DC + c) * S, (par * DC + c + 1) * S) for c in range(DC)]
                three(bank[:, 0:S], [(wq_ap(w_hi, c, hp), wq_ap(w_lo, c, hp), xt_hi[:, s[c]], xt_lo[:, s[c]])
                                      for c in range(DC)])
                three(bank[:, S:2 * S], [(wk_ap(w_hi, c, hp), wk_ap(w_lo, c, hp), ct_hi[:, s[c]], ct_lo[:, s[c]])
                                          for c in range(DC)]).then_inc(qk_done, 1)

            def project_v(jb, hf, kt, par):
                wait(pe, m_free, jb)
                s = [slice((par * DC + c) * S + kt * P, (par * DC + c) * S + (kt + 1) * P) for c in range(DC)]
                three(m_ps[:, :], [(ct_hi[:, s[c]], ct_lo[:, s[c]], wv_ap(w_hi, c, hf), wv_ap(w_lo, c, hf))
                                       for c in range(DC)]).then_inc(m_done, 1)

            def transposes(jb, src):
                wait(pe, m_free, jb)
                for t in range(TB):
                    for c in range(DC):
                        last = nc.tensor.transpose(m_ps[:, c * S + t * P:c * S + (t + 1) * P],
                                                   src[:, t * D + c * P:t * D + (c + 1) * P], ident[:, :])
                last.then_inc(m_done, 1)

            def scores(u, slot, j):
                wait(pe, exp_done, 2 * (u - 1) + j + 1)
                for t in range(TB):
                    q = qst(slot, j)[:, t * P:(t + 1) * P]
                    mm(s_ps[j][:, t * S:(t + 1) * S], q, kmv(slot, j, 0), start=True, stop=False)
                    last = mm(s_ps[j][:, t * S:(t + 1) * S], q, kmv(slot, j, 1), start=False, stop=True)
                last.then_inc(s_done, 1)

            def transpose_p(u, par, j):
                pe.wait_ge(norm_done, 2 * u + j + 1)
                wait(pe, pt_done, 2 * (u - 1) + j + 1)
                slot = 2 * par + j
                for t in range(TB):
                    for kt in range(TB):
                        c = (slot * TB + t) * S + kt * P
                        last = nc.tensor.transpose(t_ps[j][:, kt * S + t * P:kt * S + (t + 1) * P],
                                                   p_sb[:, c:c + P], ident[:, :])
                last.then_inc(t_done, 1)

            def attend(u, hp):
                wait(pe, pt_done, 2 * u + 2)
                wait(pe, ol_done, u)
                hf, q4 = hp // 4, hp % 4
                for kt in range(TB):
                    for j in range(2):
                        c = (hf * TB + kt) * CH + q4 * P + j * DH
                        last = mm(o_ps[half(j), 0:S], v_sb[:, c:c + DH],
                                  pt_sb[:, (j * TB + kt) * S:(j * TB + kt + 1) * S],
                                  start=(kt == 0), stop=(kt == TB - 1))
                last.then_inc(pv_done, 1)

            def project_out(jb, t, p):
                wait(pe, m_free, jb)
                terms = []
                for hp in range(HP):
                    s = slice(o_cols(p, hp) + t * P, o_cols(p, hp) + (t + 1) * P)
                    terms.append((o_hi[:, s], o_lo[:, s], wo_ap(wo_hi, hp), wo_ap(wo_lo, hp)))
                three(m_ps[:, 0:D], terms).then_inc(m_done, 1)

            def router(jb):
                wait(pe, m_free, jb)
                for t in range(TB):
                    for c in range(DC):
                        last = mm(m_ps[:, t * E:(t + 1) * E], xt_f[:, c * S + t * P:c * S + (t + 1) * P],
                                  wr_c[:, c * E:(c + 1) * E], start=(c == 0), stop=(c == DC - 1))
                last.then_inc(m_done, 1)

            def rank(b, jb):
                wait(pe, m_free, jb)
                pe.wait_ge(hot_done, b + 1)
                mm(m_ps[:, 0:TB * E], upper[:, :], hot[:, :], start=True, stop=True)
                mm(m_ps[:, TB * E:2 * TB * E], ones_pp[:, :], hot[:, :], start=True, stop=True).then_inc(m_done, 1)

            pe.wait_ge(consts_set, 2)
            pe.wait_ge(xn_done, 1)
            transposes(job(-1, "px"), xn[:, :])
            pe.wait_ge(c_sem, 16)
            transposes(job(-1, "pc"), c_in[:, :])
            pe.wait_ge(wlo_done, len(SPLIT_FIRST))
            pe.wait_ge(xt_done, 1)
            pe.wait_ge(m_free, 2)
            for u in range(AHEAD - 1):
                project_qk(u, u, 0)
            pe.wait_ge(gate_in, 64)
            pe.wait_ge(vo_lo_done, CO - CV)
            project_v(job(-1, "v0a"), 0, 0, 0)
            project_v(job(-1, "v0b"), 0, 1, 0)
            pe.wait_ge(dup_done[0], 32)
            scores(0, 0, 0)
            scores(0, 0, 1)
            project_qk(AHEAD - 1, AHEAD - 1, 0)
            pe.wait_ge(wlo_done, CV)

            def body(b, p, b_half):
                first, last = is_first(b), is_last(b)
                for hp in range(HP):
                    u = 8 * b + hp
                    if hp == 3 and not last:
                        pe.wait_ge(xn_done, b + 2)
                        transposes(job(b, "px"), xn[:, :])
                    if not first:
                        if hp == 4:
                            pe.wait_ge(xf_done, b)
                            transposes(job(b, "tf"), xf[:, :])
                        if hp == 5:
                            router(job(b, "lg"))
                        if hp == 6:
                            rank(b - 1, job(b, "rk"))
                    if not (first and hp == 0):
                        transpose_p(u - 1, (hp + 1) % 2, 0)
                        transpose_p(u - 1, (hp + 1) % 2, 1)
                    if not (last and hp == HP - 1):
                        slot = (hp + 1) % QS
                        pe.wait_ge(dup_done[slot], 32 * (b * (HP // QS) + (hp + 1) // QS + 1))
                        scores(u + 1, slot, 0)
                        scores(u + 1, slot, 1)
                    if hp in (1, 2) and not first:
                        if hp == 1:
                            pe.wait_ge(ol_done, u - 1)
                            pe.wait_ge(vo_lo_done, WCH - CV)
                        project_out(job(b, f"out{hp - 1}"), hp - 1, 1 - p)
                    if hp == 0 and not last:
                        pe.wait_ge(c_sem, 16 * (b + 2))
                        transposes(job(b, "pc"), c_in[:, :])
                    if hp in (3, 4):
                        project_v(job(b, f"v1{'ab'[hp - 3]}"), 1, hp - 3, p)
                    if hp in (5, 6) and not last:
                        project_v(job(b, f"v0{'ab'[hp - 5]}"), 0, hp - 5, 1 - p)
                    if hp == 1:
                        pe.wait_ge(m_free, job(b - 1, "v0b") + 1)
                    if hp == 5:
                        pe.wait_ge(m_free, job(b, "v1b") + 1)
                    if not (first and hp == 0):
                        attend(u - 1, (hp - 1) % HP)
                    if not last or hp + AHEAD < HP:
                        nxt = hp + AHEAD >= HP
                        if hp + AHEAD == HP:
                            pe.wait_ge(xt_done, b + 2)
                            pe.wait_ge(m_free, job(b, "pc") + 1)
                        project_qk(u + AHEAD, (hp + AHEAD) % HP, (1 - p) if nxt else p)

            batches(body, pe)
            for j in range(2):
                transpose_p(B * HP - 1, 1, j)
            attend(B * HP - 1, HP - 1)
            pe.wait_ge(ol_done, B * HP)
            project_out(job(B, "out0"), 0, 1)
            project_out(job(B, "out1"), 1, 1)

            pe.wait_ge(xf_done, B)
            transposes(job(B, "tf"), xf[:, :])
            router(job(B, "lg"))
            rank(B - 1, job(B, "rk"))

            def expert_of(n):
                return pe.value_load(g_i[0:1, n:n + 1] if isinstance(n, int) else g_i[0:1, bass.ds(n, 1)],
                                     min_val=0, max_val=E - 1)

            def x_in_tile(n, par):
                pe.wait_ge(xfg_done, n + 1)
                wait(pe, xgt_done, n - 1)
                for c in range(DC):
                    last = nc.tensor.transpose(xt_ps[par][:, c * P:(c + 1) * P],
                                               xfg[:, par * D + c * P:par * D + (c + 1) * P], ident[:, :])
                last.then_inc(xgt_ps_done, 1)

            def up(n, par, ex, c):
                pe.wait_ge(xgt_done, n + 1)
                wait(pe, h1_done, 2 * (n - 1) + c + 1)
                for k in range(DC):
                    last = mm(h_ps[c][:, :], xgt[:, (par * DC + k) * P:(par * DC + k + 1) * P],
                              w1_raw[:, bass.ds(ex * (DC * F) + (k * F + c * CH), CH)],
                              start=(k == 0), stop=(k == DC - 1))
                last.then_inc(h_done, 1)

            def hidden_t(n, par):
                for c in range(2):
                    pe.wait_ge(h1_done, 2 * n + c + 1)
                    for k in range(CH // P):
                        col = par * F + c * CH + k * P
                        last = nc.tensor.transpose(ht_ps[c][:, k * P:(k + 1) * P], h1[:, col:col + P], ident[:, :])
                    last.then_inc(ht_done, 1)

            def down(n, par, ex):
                pe.wait_ge(h1t_done, 2 * n + 2)
                for k in range(FC):
                    last = mm(y_ps[par][:, 0:D], h1t[:, par * F + k * P:par * F + (k + 1) * P],
                              w2_raw[:, bass.ds(ex * (FC * D) + k * D, D)], start=(k == 0), stop=(k == FC - 1))
                last.then_inc(y_done, 1)

            pe.wait_ge(plan_done, 1)
            pe.wait_ge(w1_in, 16 * E)
            x_in_tile(0, 0)
            x_in_tile(1, 1)
            for c in range(2):
                up(0, 0, expert_of(0), c)
            pe.wait_ge(w2_in, 16)

            def step(n, par, n_half, last):
                if not last:
                    nxt = expert_of(n + 1)
                    up(n + 1, 1 - par, nxt, 0)
                hidden_t(n, par)
                if not (last or isinstance(n, int) and n + 2 >= NG):
                    x_in_tile(n + 2, par)
                if not last:
                    up(n + 1, 1 - par, nxt, 1)
                down(n, par, expert_of(n))

            expert_tiles(step, pe)


def kernel(x, ctx_1024, L0_xattn_ln_gamma, L0_xattn_ln_beta, L0_xattn_w_q, L0_xattn_w_kv, L0_xattn_w_out,
           L0_xattn_b_out, L0_xattn_gate, L0_ffn_Wr, L0_ffn_br, L0_ffn_We1, L0_ffn_be1, L0_ffn_We2, L0_ffn_be2):
    import numpy as np
    import concourse.bacc as bacc
    from concourse.bass_utils import run_bass_kernel_spmd

    ins = {
        "x": x, "ctx": ctx_1024,
        "ln_gamma": np.asarray(L0_xattn_ln_gamma).reshape(DC, P).T, "ln_beta": np.asarray(L0_xattn_ln_beta).reshape(DC, P).T,
        "w_q": L0_xattn_w_q, "w_kv": L0_xattn_w_kv, "w_out": L0_xattn_w_out, "b_out": L0_xattn_b_out,
        "gate": L0_xattn_gate, "w_router": L0_ffn_Wr, "b_router": L0_ffn_br,
        "we1": L0_ffn_We1, "be1": L0_ffn_be1, "we2": L0_ffn_We2, "be2": L0_ffn_be2,
    }
    nc = bacc.Bacc("TRN2", target_bir_lowering=False, num_devices=1)
    arrays, args = {}, []
    for name, a in ins.items():
        a = np.ascontiguousarray(a)
        arrays["in_" + name] = a
        args.append(nc.dram_tensor("in_" + name, a.shape, mybir.dt.from_np(a.dtype), kind="ExternalInput").ap())
    args.append(nc.dram_tensor("out_x", (B, S, D), F32, kind="ExternalOutput").ap())
    attention_and_routed_ffn(nc, *args)
    r = run_bass_kernel_spmd(nc, [arrays], core_ids=[0])
    return r.results[0]["out_x"]
```

```python
import concourse.bass as bass
from concourse import mybir
from contextlib import ExitStack

F32 = mybir.dt.float32
F32R = mybir.dt.float32r
I32 = mybir.dt.int32
U32 = mybir.dt.uint32
ACT = mybir.ActivationFunctionType
ALU = mybir.AluOpType
AX = mybir.AxisListType

B, S, D = 8, 256, 256
H, DH = 16, 64
INNER = H * DH
E, F = 4, 1024
P = 128
EPS = 1e-5
SCALE = DH ** -0.5

HP = H // 2
TB = S // P
NT = B * TB
DC = D // P
FC = F // P
CH = 512
QS = 4
AHEAD = 4
WCH = (3 * D * INNER + INNER * D) // P // CH
CQ, CK, CV, CO = 0, 4, 8, 12
NG = NT + E - 1
RW = D + 3
REG = B * S + P
PAD = S + P
ROWS = E * REG + (E - 1) * P


def attention_and_routed_ffn(nc, x, ctx, gamma, beta, w_q, w_kv, w_out, b_out, gate,
                             w_rt, b_r, we1, be1, we2, be2, out):
    rows_dram = nc.dram_tensor("expert_rows", (ROWS, RW), F32, kind="Internal").ap()
    es = ExitStack()
    with es:
        def sem(name):
            return es.enter_context(nc.semaphore(name))

        def keep(name, shape, dt=F32):
            return es.enter_context(nc.sbuf_tensor(name, shape, dt))

        x_all = keep("x_all", [P, NT * D])
        ident = keep("ident", [P, P])
        gamma_c = keep("gamma_c", [P, DC])
        beta_c = keep("beta_c", [P, DC])
        eps_c = keep("eps_c", [P, TB])
        mhalf_c = keep("mhalf_c", [P, TB])
        gate_c = keep("gate_c", [P, 1])
        tanh_c = keep("tanh_c", [P, 1])
        br_c = keep("br_c", [P, E])
        wr_c = keep("wr_c", [P, DC * E])
        ids = keep("ids", [P, NT], I32)
        run = keep("run", [P, E])
        run_i = keep("run_i", [P, E], I32)
        w1_lo = keep("w1_lo", [P, E * DC * F], F32R)
        w1_raw = w1_lo[:, :].bitcast(F32)

        phase_a = ExitStack()

        def a_sb(name, shape, dt=F32):
            return phase_a.enter_context(nc.sbuf_tensor(name, shape, dt))

        w_hi = a_sb("w_hi", [P, CO * CH], F32R)
        w_lo = a_sb("w_lo", [P, CO * CH], F32R)
        xt_hi = a_sb("xt_hi", [P, 2 * DC * S], F32R)
        xt_lo = a_sb("xt_lo", [P, 2 * DC * S], F32R)
        ct_hi = a_sb("ct_hi", [P, 2 * DC * S], F32R)
        ct_lo = a_sb("ct_lo", [P, 2 * DC * S], F32R)
        wo_hi = a_sb("wo_hi", [P, (WCH - CO) * CH], F32R)
        wo_lo = a_sb("wo_lo", [P, (WCH - CO) * CH], F32R)
        q_st = a_sb("q_st", [P, QS * 2 * S], F32R)
        k_mv = a_sb("k_mv", [P, QS * 2 * 2 * S], F32R)
        v_sb = a_sb("v_sb", [P, 2 * TB * CH])
        c_in = a_sb("c_in", [P, TB * D])
        p_sb = a_sb("p_sb", [P, 4 * TB * S])
        pt_sb = a_sb("pt_sb", [P, 2 * TB * S])
        o_hi = a_sb("o_hi", [P, (HP + 2) * S], F32R)
        o_lo = a_sb("o_lo", [P, (HP + 2) * S], F32R)
        xn = a_sb("xn", [P, TB * D])
        xt_f = a_sb("xt_f", [P, DC * S])
        xf = a_sb("xf", [P, TB * D])
        stage = a_sb("stage", [P, 2 * TB * RW])
        bo_b = a_sb("bo_b", [P, D])
        neg_max = a_sb("neg_max", [P, 4 * TB])
        row_sum = a_sb("row_sum", [P, 4 * TB])
        inv_sum = a_sb("inv_sum", [P, 4 * TB])
        bst = a_sb("bst", [P, TB * 6])
        mv = a_sb("mv", [P, TB * 2])
        rstd = a_sb("rstd", [P, TB])
        var_e = a_sb("var_e", [P, TB])
        bst3 = a_sb("bst3", [P, TB * 6])
        mv3 = a_sb("mv3", [P, TB * 2])
        var_e3 = a_sb("var_e3", [P, TB])
        rstd3 = a_sb("rstd3", [P, TB])
        empty = xn[:, 0:RW]
        lgb = a_sb("lgb", [P, TB * E])
        best = a_sb("best", [P, TB])
        eq = a_sb("eq", [P, TB * E])
        score = a_sb("score", [P, TB * E])
        top = a_sb("top", [P, TB])
        hot = a_sb("hot", [P, TB * E])
        rkc = a_sb("rkc", [P, 2 * TB * E])
        off1 = a_sb("off1", [P, E])
        pos4 = a_sb("pos4", [P, TB * E])
        pos4h = a_sb("pos4h", [P, TB * E])
        pos_f = a_sb("pos_f", [P, TB])
        pos_i = a_sb("pos_i", [P, 2 * TB], I32)
        e_w = a_sb("e_w", [P, E])
        upper = a_sb("upper", [P, P])
        ones_pp = a_sb("ones_pp", [P, P])

        phase_a.close()

        def f_sb(name, shape, dt=F32):
            return keep(name, shape, dt)

        w1_hi = f_sb("w1_hi", [P, E * DC * F], F32R)
        w2_lo = f_sb("w2_lo", [P, E * FC * D], F32R)
        w2_raw = w2_lo[:, :].bitcast(F32)
        w2_hi = f_sb("w2_hi", [P, E * FC * D], F32R)
        b1_b = x_all
        assert NT * D == E * F
        b2_b = f_sb("b2_b", [P, E * D])
        ones_e = f_sb("ones_e", [P, E])
        n_f = f_sb("n_f", [P, E])
        n_i = f_sb("n_i", [P, E], I32)
        t_i = f_sb("t_i", [P, E], I32)
        t_f = f_sb("t_f", [P, E])
        t_inc = f_sb("t_inc", [P, E])
        skip = f_sb("skip", [P, E])
        reg0 = f_sb("reg0", [P, E])
        g_io = f_sb("g_io", [P, NG])
        g_ge = f_sb("g_ge", [P, (E - 1) * NG])
        g_sk = f_sb("g_sk", [P, E * NG])
        g_ex = f_sb("g_ex", [P, NG])
        g_row = f_sb("g_row", [P, NG])
        g_i = f_sb("g_i", [P, NG], I32)
        g_r = f_sb("g_r", [P, NG], I32)
        xg = f_sb("xg", [P, 2 * RW])
        xfg = f_sb("xfg", [P, 2 * D])
        xgt_hi = f_sb("xgt_hi", [P, 2 * DC * P], F32R)
        xgt_lo = f_sb("xgt_lo", [P, 2 * DC * P], F32R)
        h1 = f_sb("h1", [P, 2 * F])
        h1t_hi = f_sb("h1t_hi", [P, 2 * F], F32R)
        h1t_lo = f_sb("h1t_lo", [P, 2 * F], F32R)
        xb2 = f_sb("xb2", [P, 2 * D])
        idx = f_sb("idx", [P, 2], I32)
        y_sb = f_sb("y_sb", [P, 2 * D])

        banks = [es.enter_context(nc.psum_tensor(f"bank{n}", [P, CH], F32)) for n in range(8)]
        s_ps = banks[0:2]
        t_ps = banks[2:4]
        o_ps = banks[4]
        qk_ps = banks[5:7]
        m_ps = banks[7]
        out_ps = (m_ps, qk_ps[0])
        h_ps = banks[0:2]
        ht_ps = banks[2:4]
        y_ps = banks[4:6]
        xt_ps = banks[6:8]

        x_in, x_rest_in, wq_in, wk_in, wv_in, wo_in, consts_in, gate_in, b1_in = (
            sem(n) for n in ("x_in", "x_rest_in", "wq_in", "wk_in", "wv_in", "wo_in", "consts_in", "gate_in", "b1_in"))
        c_sem, wqk_rest_in = sem("ctx_in"), sem("wqk_rest_in")
        w1_in, w2_in = sem("w1_in"), sem("w2_in")
        consts_set, tanh_done, xb_done = sem("consts_set"), sem("tanh_done"), sem("xb_done")
        whi_done, wlo_done = sem("whi_done"), sem("wlo_done")
        vo_lo_done = sem("vo_lo_done")
        qk_done, qk_hi, qk_lo = sem("qk_done"), sem("qk_hi"), sem("qk_lo")
        dup_done = [sem(f"dup_done{n}") for n in range(QS)]
        s_done, mx_done, exp_done, norm_done = sem("s_done"), sem("mx_done"), sem("exp_done"), sem("norm_done")
        inv_done = sem("inv_done")
        t_done, pt_done, pv_done = sem("t_done"), sem("pt_done"), sem("pv_done")
        oh_done, ol_done = sem("oh_done"), sem("ol_done")
        m_done, m_free = sem("m_done"), sem("m_free")
        var_done, rstd_done, xn_done = sem("var_done"), sem("rstd_done"), sem("xn_done")
        xth_done, xt_done = sem("xth_done"), sem("xt_done")
        cth_done = sem("cth_done")
        var3_done, rstd3_done = sem("var3_done"), sem("rstd3_done")
        dve_chain = sem("dve_chain")
        dve_passed = sem("dve_passed")
        pool_chain = sem("pool_chain")
        pool_passed = sem("pool_passed")
        phase_a_left, empty_row_made = sem("phase_a_left"), sem("empty_row_made")
        xf_done, hot_done, pos_done = sem("xf_done"), sem("hot_done"), sem("pos_done")
        plan_done, idx_done, xfg_done = sem("plan_done"), sem("idx_done"), sem("xfg_done")
        run_done, padded = sem("run_done"), sem("padded")
        sent = [sem(f"sent{n}") for n in range(2)]
        xg_in = [sem(f"xg_in{n}") for n in range(2)]
        f1_hi_done, f1_lo_done = sem("f1_hi_done"), sem("f1_lo_done")
        f2_hi_done, f2_lo_done = sem("f2_hi_done"), sem("f2_lo_done")
        xgt_ps_done, xgt_hi_done, xgt_lo_done = sem("xgt_ps_done"), sem("xgt_hi_done"), sem("xgt_lo_done")
        h_done, h1_done, ht_done = sem("h_done"), sem("h1_done"), sem("ht_done")
        h1t_hi_done, h1t_lo_done = sem("h1t_hi_done"), sem("h1t_lo_done")
        y_done, ysb_done, xb2_done = sem("y_done"), sem("ysb_done"), sem("xb2_done")
        stored = [sem(f"stored{n}") for n in range(2)]

        block = es.enter_context(nc.Block())

        def wait(eng, s, value):
            if not (isinstance(value, int) and value <= 0):
                eng.wait_ge(s, value)

        BEFORE = ("px", "pc", "v0a", "v0b")
        FIRST = ("pc", "px", "v1a", "v1b", "v0a", "v0b")
        JOBS = ("pc", "out0", "out1", "px", "v1a", "v1b", "tf", "v0a", "lg", "v0b", "rk")
        LAST = ("out0", "out1", "v1a", "v1b", "tf", "lg", "rk")
        AFTER = ("out0", "out1", "tf", "lg", "rk")

        def job(b, name):
            if isinstance(b, int):
                lists = [BEFORE, FIRST] + [JOBS] * (B - 2) + [LAST, AFTER]
                return sum(len(l) for l in lists[:b + 1]) + lists[b + 1].index(name)
            return len(BEFORE) + len(FIRST) + len(JOBS) * (b - 1) + JOBS.index(name)

        def wq_ap(w, dc, hp):
            c = (CQ + 2 * dc) * CH + hp * P
            return w[:, c:c + P]

        def wk_ap(w, dc, hp):
            c = (CK + 2 * dc) * CH + hp * P
            return w[:, c:c + P]

        def wv_ap(w, dc, half):
            c = (CV + 2 * dc + half) * CH
            return w[:, c:c + CH]

        def wo_ap(w, hp):
            return w[:, hp * D:(hp + 1) * D]

        SPLIT_FIRST = (CQ, CQ + 2, CK, CK + 2)
        SPLIT_THEN = (CQ + 1, CQ + 3, CK + 1, CK + 3)
        SPLIT = SPLIT_FIRST + SPLIT_THEN + tuple(range(CV, WCH))

        def chunk(w, wo, c):
            return w[:, c * CH:(c + 1) * CH] if c < CO else wo[:, (c - CO) * CH:(c - CO + 1) * CH]

        FCH = E * DC * F // CH
        FCH_DVE = 7
        FCH_POOL = 8

        def ffn_chunk(w, c):
            return w[:, c * CH:(c + 1) * CH]

        def stage_ap(p, t, a, z):
            c = (p * TB + t) * RW
            return stage[:, c + a:c + z]

        def stage_col(p, k):
            return stage[:, p * TB * RW:(p + 1) * TB * RW].rearrange("p (t k) -> p t k", t=TB)[:, :, k:k + 1]

        def qst(slot, j):
            return q_st[:, (2 * slot + j) * S:(2 * slot + j + 1) * S]

        def kmv(slot, j, part):
            c = ((2 * slot + j) * 2 + part) * S
            return k_mv[:, c:c + S]

        def o_cols(p, hp):
            c = (hp if hp >= 2 or p == 0 else HP + hp) * S
            return c

        def half(j):
            return slice(DH * j, DH * j + DH)

        def batches(eng_body, eng):
            eng_body(0, 0, 0)
            with eng.Fori(0, (B - 2) // 2) as i:
                eng_body(2 * i + 1, 1, i)
                eng_body(2 * i + 2, 0, i + 1)
            eng_body(B - 1, 1, (B - 1) // 2)

        def is_first(b):
            return isinstance(b, int) and b == 0

        def is_last(b):
            return isinstance(b, int) and b == B - 1

        def expert_tiles(step, eng):
            step(0, 0, 0, False)
            step(1, 1, 0, False)
            with eng.Fori(1, NG // 2 - 1) as i:
                step(2 * i, 0, i, False)
                step(2 * i + 1, 1, i, False)
            assert NG % 2
            for n in range(NG - 3, NG):
                step(n, n % 2, n // 2, n == NG - 1)

        @block.sync
        def _(sp):
            sp.dma_start(x_all[:, 0:TB * D].rearrange("p (t d) -> p t d", d=D),
                         x[0].rearrange("(t p) d -> p t d", p=P)).then_inc(x_in, 16)
            sp.dma_start(c_in[:, :].rearrange("p (t d) -> p t d", d=D),
                         ctx[0].rearrange("(t p) d -> p t d", p=P)).then_inc(c_sem, 16)
            raw = w1_raw

            def load_half(first_chunk, src, k, arrived):
                cols = raw[:, first_chunk * CH:(first_chunk + 4) * CH].rearrange("p (c k n) -> p c k n", c=DC, k=2)
                sp.dma_start(cols[:, :, k, :], src.rearrange("(c p) (k n) -> k p c n", p=P, k=2)[k]).then_inc(arrived, 16)

            load_half(CQ, w_q, 0, wq_in)
            load_half(CK, w_kv[:, 0:INNER], 0, wk_in)
            sp.dma_start(gamma_c[:, :], gamma).then_inc(consts_in, 16)
            sp.dma_start(beta_c[:, :], beta).then_inc(consts_in, 16)
            load_half(CQ, w_q, 1, wqk_rest_in)
            load_half(CK, w_kv[:, 0:INNER], 1, wqk_rest_in)
            sp.dma_start(raw[:, CV * CH:CO * CH].rearrange("p (c n) -> p c n", c=DC),
                         w_kv[:, INNER:].rearrange("(c p) n -> p c n", p=P)).then_inc(wv_in, 16)
            sp.dma_start(raw[:, CO * CH:WCH * CH].rearrange("p (c n) -> p c n", c=HP),
                         w_out.rearrange("(c p) n -> p c n", p=P)).then_inc(wo_in, 16)
            sp.dma_start(gate_c[:, :], gate.partition_broadcast(P)).then_inc(gate_in, 16)
            sp.dma_start(bo_b[:, :], b_out.partition_broadcast(P)).then_inc(gate_in, 16)
            sp.dma_start(br_c[:, :], b_r.partition_broadcast(P)).then_inc(gate_in, 16)
            sp.dma_start(wr_c[:, :].rearrange("p (c e) -> p c e", c=DC),
                         w_rt.rearrange("(c p) e -> p c e", p=P)).then_inc(gate_in, 16)
            sp.dma_start(x_all[:, TB * D:].rearrange("p (t d) -> p t d", d=D),
                         x[1:].rearrange("b (t p) d -> p (b t) d", p=P)).then_inc(x_rest_in, 16)
            sp.wait_ge(m_done, job(-1, "pc") + 1)
            sp.dma_start(c_in[:, :].rearrange("p (t d) -> p t d", d=D),
                         ctx[1].rearrange("(t p) d -> p t d", p=P)).then_inc(c_sem, 16)

            def dup(u, slot):
                sp.wait_ge(qk_lo, u + 1)
                for j in range(2):
                    c = (2 * slot + j) * 2 * S
                    sp.dma_start(k_mv[half(1 - j), c:c + 2 * S].bitcast(F32),
                                 k_mv[half(j), c:c + 2 * S].bitcast(F32)).then_inc(dup_done[slot], 16)

            dup(0, 0)
            dup(1, 1)
            dup(2, 2)

            def body(b, p, b_half):
                u0 = 8 * b
                for hp in range(HP):
                    if not is_last(b) or hp + 3 < HP:
                        dup(u0 + hp + 3, (hp + 3) % QS)
                    if hp == 1 and not (isinstance(b, int) and b >= B - 2):
                        sp.wait_ge(m_done, job(b, "pc") + 1)
                        nb = b + 2
                        src = ctx[nb] if isinstance(b, int) else ctx[bass.ds(nb, 1)].rearrange("o r d -> (o r) d")
                        sp.dma_start(c_in[:, :].rearrange("p (t d) -> p t d", d=D),
                                     src.rearrange("(t p) d -> p t d", p=P)).then_inc(c_sem, 16)

            body(0, 0, 0)
            with sp.Fori(0, (B - 2) // 2 - 1) as i:
                body(2 * i + 1, 1, i)
                body(2 * i + 2, 0, i + 1)
            for b in range(B - 3, B):
                body(b, b % 2, b // 2)

            def pad(first_row, rows):
                sp.dma_start(rows_dram[first_row, :].rearrange("(g p) d -> p g d", p=P),
                             empty[:, :].unsqueeze(1).broadcast_to((P, rows // P, RW))).then_inc(padded, 16)

            sp.wait_ge(empty_row_made, 1)
            pad(slice(E * REG, ROWS), (E - 1) * P)
            sp.wait_ge(run_done, 1)
            for e in range(E):
                row = sp.value_load(run_i[0:1, e:e + 1], min_val=0, max_val=ROWS - PAD)
                pad(bass.ds(row, PAD), PAD)

            sp.wait_ge(phase_a_left, 1)
            sp.dma_start(b1_b[:, (E - 1) * F:], be1[E - 1].partition_broadcast(P)).then_inc(b1_in, 16)
            sp.dma_start(b2_b[:, :], be2.rearrange("e n -> (e n)").partition_broadcast(P)).then_inc(b1_in, 16)

            def load_rows(n, par):
                row = sp.value_load(g_r[0:1, n:n + 1] if isinstance(n, int) else g_r[0:1, bass.ds(n, 1)],
                                    min_val=0, max_val=ROWS - P)
                sp.dma_start(xg[:, par * RW:(par + 1) * RW], rows_dram[bass.ds(row, P), :]).then_inc(xg_in[par], 16)

            sp.wait_ge(plan_done, 1)
            for n in range(2):
                sp.wait_ge(sent[n], 32 * (B // 2))
            load_rows(0, 0)
            load_rows(1, 1)
            with sp.Fori(0, NG // 2 - 1) as i:
                for par in range(2):
                    n = 2 * i + par
                    sp.wait_ge(xfg_done, n + 1)
                    sp.wait_ge(idx_done, n + 1)
                    load_rows(n + 2, par)
            sp.wait_ge(xfg_done, NG - 2)
            sp.wait_ge(idx_done, NG - 2)
            load_rows(NG - 1, 0)
            for n in range(2):
                sp.wait_ge(stored[n], 16 * ((NG + 1 - n) // 2))

        @block.gpsimd
        def _(pool):
            g = nc.gpsimd
            count = [0]

            def link(ins):
                count[0] += 1
                ins.then_inc(pool_chain, 1)
                pool.wait_ge(pool_chain, count[0])

            g.iota(ids[:, :], [[P, NT]], base=0, channel_multiplier=1)
            g.memset(eps_c[:, :], EPS)
            g.memset(mhalf_c[:, :], -0.5)
            link(g.memset(ident[:, :], 0.0))
            g.affine_select(out=ident[:, :], in_=ident[:, :], compare_op=ALU.not_equal, fill=1.0, base=0,
                            pattern=[[-1, P]], channel_multiplier=1).then_inc(consts_set, 1)
            g.iota(e_w[:, :], [[-1, E]], base=E, channel_multiplier=0, allow_small_or_imprecise_dtypes=True)
            g.iota(run[:, :], [[REG, E]], base=0, channel_multiplier=0, allow_small_or_imprecise_dtypes=True)
            link(g.memset(ones_pp[:, :], 1.0))
            g.affine_select(out=upper[:, :], in_=ones_pp[:, :], compare_op=ALU.is_gt, fill=0.0, base=0,
                            pattern=[[1, P]], channel_multiplier=-1).then_inc(consts_set, 1)

            def make_empty_row():
                pool.wait_ge(m_done, job(B - 2, "px") + 1)
                link2(g.memset(empty[:, :], 0.0))
                g.iota(empty[:, RW - 1:RW].bitcast(I32), [[0, 1]], base=B * S,
                       channel_multiplier=1).then_inc(empty_row_made, 1)

            def send(b, p, b_half):
                wait(pool, pos_done, b + 1)
                pool.sem_inc(pool_passed, 1)
                for t in range(TB):
                    g.indirect_dma_start(out=rows_dram[:, :],
                                         out_offset=bass.IndirectOffsetOnAxis(
                                             ap=pos_i[:, p * TB + t:p * TB + t + 1].bitcast(U32), axis=0),
                                         in_=stage_ap(p, t, 0, RW), in_offset=None).then_inc(sent[p], 16)

            def rstd_step(src, tmp, dst, ready, value, done):
                wait(pool, ready, value)
                link2(g.tensor_tensor(tmp[:, :], src[:, 1:2 * TB:2], eps_c[:, :], ALU.add))
                g.tensor_tensor(dst[:, :], tmp[:, :], mhalf_c[:, :], ALU.pow).then_inc(done, 1)

            def add_b_out(b):
                pool.wait_ge(xn_done, b + 1)
                n = TB * D
                xb = x_all[:, b * n:b * n + n] if isinstance(b, int) else x_all[:, bass.ds(b * n, n)]
                xb = xb.rearrange("p (t d) -> p t d", t=TB)
                g.tensor_tensor(xb, xb, bo_b[:, :].unsqueeze(1).broadcast_to((P, TB, D)), ALU.add).then_inc(xb_done, 1)

            def b_out_gated():
                pool.wait_ge(tanh_done, 1)
                pool.wait_ge(gate_in, 64)
                link2(g.tensor_scalar(bo_b[:, :], bo_b[:, :], tanh_c[:, 0:1], None, ALU.mult))

            def normalise(u, par, j):
                pool.wait_ge(inv_done, 2 * u + j + 1)
                slot = 2 * par + j
                pv = p_sb[:, slot * TB * S:(slot + 1) * TB * S].rearrange("p (t k) -> p t k", t=TB)
                rs = inv_sum[:, slot * TB:(slot + 1) * TB].unsqueeze(2).broadcast_to((P, TB, S))
                g.tensor_tensor(pv, pv, rs, ALU.mult).then_inc(norm_done, 1)

            chain = {"base": count[0], "n": 0}
            PER_BATCH = 3

            def link2(ins):
                chain["n"] += 1
                ins.then_inc(pool_chain, 1)
                pool.wait_ge(pool_chain, chain["base"] + chain["n"])

            pool.wait_ge(consts_set, 1)
            rstd_step(mv, var_e, rstd, var_done, 1, rstd_done)
            rstd_step(mv, var_e, rstd, var_done, 2, rstd_done)
            def split_lo(c):
                pool.wait_ge(whi_done, SPLIT.index(c) + 1)
                g.tensor_tensor(chunk(w_lo, wo_lo, c), w1_raw[:, c * CH:(c + 1) * CH],
                                chunk(w_hi, wo_hi, c).bitcast(F32), ALU.subtract).then_inc(vo_lo_done, 1)

            for c in range(CV, CO):
                split_lo(c)
            b_out_gated()
            base0 = chain["base"] + chain["n"]

            for j in range(2):
                normalise(0, 0, j)

            def body(b, p, b_half):
                first, last = is_first(b), is_last(b)
                chain["base"], chain["n"] = base0 if first else base0 + 2 + PER_BATCH * (b - 1), 0
                u0 = 8 * b
                for hp in range(HP):
                    if hp == 1 and not last:
                        rstd_step(mv, var_e, rstd, var_done, 2 * b + 3, rstd_done)
                    if not (last and hp == HP - 1):
                        for j in range(2):
                            normalise(u0 + hp + 1, (hp + 1) % 2, j)
                    if hp == 1 and not last:
                        rstd_step(mv, var_e, rstd, var_done, 2 * b + 4, rstd_done)
                    if hp == 2 and not first:
                        rstd_step(mv3, var_e3, rstd3, var3_done, b, rstd3_done)
                    if hp == 5:
                        add_b_out(b)
                    if last and hp == 0:
                        make_empty_row()
                    if first and hp < WCH - CO:
                        split_lo(CO + hp)
                    if last and hp >= 6:
                        ffn_lo(w1_lo, w1_hi, hp - 6, f1_hi_done, f1_lo_done)
                    if hp == 7 and not (first or last):
                        send(b - 1, 1 - p, b_half)

            def ffn_lo(lo, hi, c, hi_done, done):
                pool.wait_ge(hi_done, c + 1)
                g.tensor_tensor(ffn_chunk(lo, c), ffn_chunk(lo, c).bitcast(F32), ffn_chunk(hi, c).bitcast(F32),
                                ALU.subtract).then_inc(done, 1)

            batches(body, pool)
            for c in range(2, FCH - FCH_DVE - 2):
                ffn_lo(w1_lo, w1_hi, c, f1_hi_done, f1_lo_done)
            chain["base"], chain["n"] = base0 + 2 + PER_BATCH * (B - 2) + 2, 0
            rstd_step(mv3, var_e3, rstd3, var3_done, B, rstd3_done)

            pool.wait_ge(phase_a_left, 1)
            g.memset(ones_e[:, :], 1.0)
            g.iota(g_io[:, :], [[1, NG]], base=0, channel_multiplier=0, allow_small_or_imprecise_dtypes=True)
            g.iota(reg0[:, :], [[REG, E]], base=0, channel_multiplier=0,
                   allow_small_or_imprecise_dtypes=True).then_inc(consts_set, 1)
            for c in range(FCH - FCH_DVE - 2, FCH - FCH_DVE):
                ffn_lo(w1_lo, w1_hi, c, f1_hi_done, f1_lo_done)
            send(B - 2, 0, 0)
            pool.wait_ge(padded, 16 * (E + 1))
            send(B - 1, 1, 0)
            for c in range(FCH - FCH_POOL, FCH):
                ffn_lo(w2_lo, w2_hi, c, f2_hi_done, f2_lo_done)

            def expert_of(n):
                return pool.value_load(g_i[0:1, n:n + 1] if isinstance(n, int) else g_i[0:1, bass.ds(n, 1)],
                                       min_val=0, max_val=E - 1)

            def tile_x(n, par, n_half, ex):
                pool.wait_ge(xg_in[par], 16 * (n_half + 1))
                wait(pool, ysb_done, n - 1)
                g.tensor_tensor(xb2[:, par * D:(par + 1) * D], xg[:, par * RW:par * RW + D],
                                b2_b[:, bass.ds(ex * D, D)], ALU.add).then_inc(xb2_done, 1)
                wait(pool, stored[par], 16 * n_half)
                pool.sem_inc(pool_passed, 1)
                g.tensor_copy(idx[:, par:par + 1],
                              xg[:, (par + 1) * RW - 1:(par + 1) * RW].bitcast(I32)).then_inc(idx_done, 1)

            pool.wait_ge(plan_done, 1)
            pool.wait_ge(b1_in, 48)
            tile_x(0, 0, 0, expert_of(0))

            def step(n, par, n_half, last):
                if not last:
                    tile_x(n + 1, 1 - par, n_half + par, expert_of(n + 1))
                pool.wait_ge(ysb_done, n + 1)
                pool.wait_ge(idx_done, n + 1)
                pool.sem_inc(pool_passed, 1)
                g.indirect_dma_start(out=out.rearrange("b s d -> (b s) d"),
                                     out_offset=bass.IndirectOffsetOnAxis(ap=idx[:, par:par + 1].bitcast(U32), axis=0),
                                     in_=y_sb[:, par * D:(par + 1) * D], in_offset=None,
                                     bounds_check=B * S - 1, oob_is_err=False).then_inc(stored[par], 16)

            expert_tiles(step, pool)

        @block.scalar
        def _(act):
            a = nc.scalar

            def split_hi(c, arrived):
                if arrived is not None:
                    act.wait_ge(arrived, 16)
                a.activation(chunk(w_hi, wo_hi, c), w1_raw[:, c * CH:(c + 1) * CH], ACT.Copy).then_inc(whi_done, 1)

            def ctx_hi(b, jb, par):
                act.wait_ge(m_done, jb + 1)
                a.activation(ct_hi[:, par * DC * S:(par + 1) * DC * S], m_ps[:, :],
                             ACT.Copy).then_inc(cth_done, 1)

            def x_hi(jb, par):
                act.wait_ge(m_free, jb + 1)
                a.activation(xt_hi[:, par * DC * S:(par + 1) * DC * S], xt_f[:, :], ACT.Copy).then_inc(xth_done, 1)

            def qk_high(u, slot):
                act.wait_ge(qk_done, u + 1)
                for j in range(2):
                    a.activation(qst(slot, j)[half(j), :], qk_ps[slot % 2][half(j), 0:S], ACT.Copy, scale=SCALE)
                for j in range(2):
                    last = a.activation(kmv(slot, j, 0)[half(j), :], qk_ps[slot % 2][half(j), S:2 * S], ACT.Copy)
                last.then_inc(qk_hi, 1)

            def exponentials(u, par, j):
                act.wait_ge(mx_done, 2 * u + j + 1)
                wait(act, t_done, 2 * (u - 2) + j + 1)
                slot = 2 * par + j
                for t in range(TB):
                    last = a.activation(p_sb[:, (slot * TB + t) * S:(slot * TB + t + 1) * S],
                                        s_ps[j][:, t * S:(t + 1) * S], ACT.Exp,
                                        bias=neg_max[:, slot * TB + t:slot * TB + t + 1],
                                        accum_out=row_sum[:, slot * TB + t:slot * TB + t + 1])
                last.then_inc(exp_done, 1)

            def evacuate_pt(u, j):
                act.wait_ge(t_done, 2 * u + j + 1)
                a.activation(pt_sb[:, j * TB * S:(j + 1) * TB * S], t_ps[j][:, :], ACT.Copy).then_inc(pt_done, 1)

            def out_high(u, p, hp):
                act.wait_ge(pv_done, u + 1)
                c = o_cols(p, hp)
                a.activation(o_hi[:, c:c + S], o_ps[:, 0:S], ACT.Copy).then_inc(oh_done, 1)

            for c in SPLIT_FIRST:
                split_hi(c, {CQ: wq_in, CK: wk_in}.get(c))
            x_hi(job(-1, "px"), 0)
            ctx_hi(0, job(-1, "pc"), 0)
            act.wait_ge(wqk_rest_in, 32)
            for c in SPLIT_THEN:
                split_hi(c, None)
            for c in range(CV, CO):
                split_hi(c, {CV: wv_in}.get(c))
            qk_high(0, 0)
            qk_high(1, 1)
            qk_high(2, 2)
            act.wait_ge(gate_in, 64)
            a.activation(tanh_c[:, :], gate_c[:, :], ACT.Tanh).then_inc(tanh_done, 1)
            for c in range(CO, WCH):
                if c == WCH - 1:
                    exponentials(0, 0, 0)
                    exponentials(0, 0, 1)
                split_hi(c, {CO: wo_in}.get(c))
            def body(b, p, b_half):
                u0 = 8 * b
                last = is_last(b)
                for hp in range(HP):
                    u = u0 + hp
                    if not (is_first(b) and hp < 2):
                        out_high(u - 2, p if hp >= 2 else 1 - p, (hp - 2) % HP)
                    if not (is_first(b) and hp == 0):
                        evacuate_pt(u - 1, 0)
                        evacuate_pt(u - 1, 1)
                    if hp == 0 and not (last or is_first(b)):
                        ctx_hi(b + 1, job(b, "pc"), 1 - p)
                    if not last or hp + 3 < HP:
                        qk_high(u + 3, (hp + 3) % QS)
                    if hp == 0 and is_first(b):
                        ctx_hi(b + 1, job(b, "pc"), 1 - p)
                    if not (last and hp == HP - 1):
                        exponentials(u + 1, (hp + 1) % 2, 0)
                        exponentials(u + 1, (hp + 1) % 2, 1)
                    if hp == 3 and not last:
                        x_hi(job(b, "px"), 1 - p)
                    if is_first(b) and hp >= WCH - CO:
                        e = hp - (WCH - CO)
                        act.wait_ge(wlo_done, CV)
                        act.wait_ge(vo_lo_done, WCH - CV)
                        act.dma_start(w1_raw[:, e * DC * F:(e + 1) * DC * F].rearrange("p (c n) -> p c n", n=F),
                                      we1[e].rearrange("(c p) n -> p c n", p=P)).then_inc(w1_in, 16)
                    if last and hp == 3:
                        act.wait_ge(m_free, job(b, "out1") + 1)
                        act.dma_start(b1_b[:, 0:(E - 1) * F],
                                      be1[0:E - 1].rearrange("e n -> (e n)").partition_broadcast(P)).then_inc(b1_in, 16)
                    if last and hp == 5:
                        act.wait_ge(m_done, job(b, "v1b") + 1)
                        act.dma_start(w2_raw[:, :].rearrange("p (ec n) -> p ec n", n=D),
                                      we2.rearrange("e (c p) n -> p (e c) n", p=P)).then_inc(w2_in, 16)
                        act.wait_ge(w1_in, 16 * E)
                    if last and hp >= 5:
                        ffn_hi(w1_hi, w1_raw, hp - 5, f1_hi_done)

            def ffn_hi(hi, raw, c, done):
                a.activation(ffn_chunk(hi, c), ffn_chunk(raw, c), ACT.Copy).then_inc(done, 1)

            batches(body, act)
            out_high(B * HP - 2, 1, HP - 2)
            evacuate_pt(B * HP - 1, 0)
            evacuate_pt(B * HP - 1, 1)
            for c in range(HP - 5, HP + 2):
                ffn_hi(w1_hi, w1_raw, c, f1_hi_done)
            out_high(B * HP - 1, 1, HP - 1)
            for c in range(HP + 2, FCH):
                ffn_hi(w1_hi, w1_raw, c, f1_hi_done)
            act.wait_ge(w2_in, 16)
            act.wait_ge(phase_a_left, 1)
            for c in range(FCH):
                ffn_hi(w2_hi, w2_raw, c, f2_hi_done)

            def xg_evacuate(n, par):
                act.wait_ge(xgt_ps_done, n + 1)
                a.activation(xgt_hi[:, par * DC * P:(par + 1) * DC * P], xt_ps[par][:, 0:DC * P],
                             ACT.Copy).then_inc(xgt_hi_done, 1)

            xg_evacuate(0, 0)
            xg_evacuate(1, 1)

            def step(n, par, n_half, last):
                for c in range(2):
                    act.wait_ge(ht_done, 2 * n + c + 1)
                    a.activation(h1t_hi[:, par * F + c * CH:par * F + (c + 1) * CH], ht_ps[c][:, :],
                                 ACT.Relu).then_inc(h1t_hi_done, 1)
                if not (last or isinstance(n, int) and n + 2 >= NG):
                    xg_evacuate(n + 2, par)

            expert_tiles(step, act)

        @block.vector
        def _(dve):
            v = nc.vector
            chain = {"base": 0, "n": 0}

            def link(ins):
                chain["n"] += 1
                ins.then_inc(dve_chain, 1)
                dve.wait_ge(dve_chain, chain["base"] + chain["n"])

            def x_tile(b, t):
                if isinstance(b, int):
                    c = (TB * b + t) * D
                    return x_all[:, c:c + D]
                return x_all[:, bass.ds((b * TB + t) * D, D)]

            def moments(src, st, dst, done):
                for t in range(TB):
                    last = v.bn_stats(st[:, 6 * t:6 * t + 6], src(t))
                link(last)
                dve.sem_inc(dve_passed, 1)
                for t in range(TB):
                    last = v.bn_aggr(dst[:, 2 * t:2 * t + 2], st[:, 6 * t:6 * t + 6])
                last.then_inc(done, 1)

            def standardise(dst, src, m, r):
                for t in range(TB):
                    last = v.tensor_scalar(dst[:, t * D:(t + 1) * D], src(t), m[:, 2 * t:2 * t + 1],
                                           r[:, t:t + 1], ALU.subtract, ALU.mult)
                return last

            def xn_tile(t):
                return xn[:, t * D:(t + 1) * D]

            def split_lo(c):
                dve.wait_ge(whi_done, SPLIT.index(c) + 1)
                v.tensor_tensor(chunk(w_lo, wo_lo, c), w1_raw[:, c * CH:(c + 1) * CH],
                                chunk(w_hi, wo_hi, c).bitcast(F32), ALU.subtract).then_inc(wlo_done, 1)

            def norm_a(b):
                moments(lambda t: x_tile(b, t), bst, mv, var_done)

            def norm_b(b):
                dve.wait_ge(rstd_done, 2 * b + 1)
                link(standardise(xn, lambda t: x_tile(b, t), mv, rstd))
                moments(xn_tile, bst, mv, var_done)

            def norm_c(b):
                dve.wait_ge(rstd_done, 2 * b + 2)
                standardise(xn, xn_tile, mv, rstd).then_inc(xn_done, 1)

            def x_affine(b, jb):
                dve.wait_ge(m_done, jb + 1)
                for c in range(DC):
                    last = v.tensor_scalar(xt_f[:, c * S:(c + 1) * S], m_ps[:, c * S:(c + 1) * S],
                                           gamma_c[:, c:c + 1], beta_c[:, c:c + 1], ALU.mult, ALU.add)
                last.then_inc(m_free, 1)

            def x_low(b, par):
                dve.wait_ge(xth_done, b + 1)
                s = slice(par * DC * S, (par + 1) * DC * S)
                v.tensor_tensor(xt_lo[:, s], xt_f[:, :], xt_hi[:, s].bitcast(F32), ALU.subtract).then_inc(xt_done, 1)

            def ctx_low(b, par):
                dve.wait_ge(cth_done, b + 1)
                s = slice(par * DC * S, (par + 1) * DC * S)
                v.tensor_tensor(ct_lo[:, s], m_ps[:, :], ct_hi[:, s].bitcast(F32),
                                ALU.subtract).then_inc(m_free, 1)

            def v_evacuate(jb, hf, kt):
                dve.wait_ge(m_done, jb + 1)
                c = (hf * TB + kt) * CH
                v.tensor_copy(v_sb[:, c:c + CH], m_ps[:, :]).then_inc(m_free, 1)

            def residual(b, p, b_half, t, jb, bank=m_ps):
                dve.wait_ge(m_done, jb + 1)
                if t == 0:
                    dve.wait_ge(xb_done, b + 1)
                    wait(dve, sent[p], 32 * b_half)
                v.scalar_tensor_tensor(out=stage_ap(p, t, 0, D), in0=bank[:, 0:D], scalar=tanh_c[:, 0:1],
                                       in1=x_tile(b, t), op0=ALU.mult, op1=ALU.add).then_inc(m_free, 1)

            def qk_low(u, slot):
                dve.wait_ge(qk_hi, u + 1)
                for j in range(2):
                    v.scalar_tensor_tensor(out=qst(slot, j)[half(1 - j), :], in0=qk_ps[slot % 2][half(j), 0:S], scalar=SCALE,
                                           in1=qst(slot, j)[half(j), :].bitcast(F32), op0=ALU.mult, op1=ALU.subtract)
                for j in range(2):
                    last = v.tensor_tensor(kmv(slot, j, 1)[half(j), :], qk_ps[slot % 2][half(j), S:2 * S],
                                           kmv(slot, j, 0)[half(j), :].bitcast(F32), ALU.subtract)
                last.then_inc(qk_lo, 1)

            def maxima(u, par, j):
                dve.wait_ge(s_done, 2 * u + j + 1)
                slot = 2 * par + j
                v.tensor_reduce(neg_max[:, slot * TB:(slot + 1) * TB],
                                s_ps[j][:, :].rearrange("p (t k) -> p t k", t=TB), AX.X, ALU.max,
                                negate=True).then_inc(mx_done, 1)

            def inverse_sums(u, par, j):
                dve.wait_ge(exp_done, 2 * u + j + 1)
                slot = 2 * par + j
                v.reciprocal(inv_sum[:, slot * TB:(slot + 1) * TB],
                             row_sum[:, slot * TB:(slot + 1) * TB]).then_inc(inv_done, 1)

            def out_low(u, p, hp):
                dve.wait_ge(oh_done, u + 1)
                s = slice(o_cols(p, hp), o_cols(p, hp) + S)
                v.tensor_tensor(o_lo[:, s], o_ps[:, 0:S], o_hi[:, s].bitcast(F32), ALU.subtract).then_inc(ol_done, 1)

            def rows(p):
                return lambda t: stage_ap(p, t, 0, D)

            def ffn_norm_a(b, p, jb):
                dve.wait_ge(m_free, jb + 1)
                moments(rows(p), bst3, mv3, var3_done)

            def ffn_norm_b(b, p):
                dve.wait_ge(rstd3_done, b + 1)
                standardise(xf, rows(p), mv3, rstd3).then_inc(xf_done, 1)
                v.tensor_copy(stage_col(p, D), mv3[:, 0::2].unsqueeze(2))
                v.tensor_copy(stage_col(p, D + 1), rstd3[:, :].unsqueeze(2))
                src = ids[:, TB * b:TB * b + TB] if isinstance(b, int) else ids[:, bass.ds(b * TB, TB)]
                v.tensor_copy(stage_col(p, D + 2).bitcast(I32), src.unsqueeze(2))

            by_expert = lambda tl: tl[:, :].rearrange("p (t e) -> p t e", e=E)

            def xf_evacuate(jb, split):
                dve.wait_ge(xt_done, split)
                dve.wait_ge(m_done, jb + 1)
                v.tensor_copy(xt_f[:, :], m_ps[:, :]).then_inc(m_free, 1)

            def logits(jb):
                dve.wait_ge(m_done, jb + 1)
                v.tensor_tensor(by_expert(lgb), m_ps[:, 0:TB * E].rearrange("p (t e) -> p t e", e=E),
                                br_c[:, :].unsqueeze(1).broadcast_to((P, TB, E)), ALU.add).then_inc(m_free, 1)

            def choose(jb):
                dve.wait_ge(m_free, jb + 1)
                link(v.tensor_reduce(best[:, :], by_expert(lgb), AX.X, ALU.max))
                link(v.tensor_tensor(by_expert(eq), by_expert(lgb),
                                     best[:, :].unsqueeze(2).broadcast_to((P, TB, E)), ALU.is_ge))
                weights = e_w[:, :].unsqueeze(1).broadcast_to((P, TB, E))
                link(v.tensor_tensor(by_expert(score), by_expert(eq), weights, ALU.mult))
                link(v.tensor_reduce(top[:, :], by_expert(score), AX.X, ALU.max))
                v.tensor_tensor(by_expert(hot), weights, top[:, :].unsqueeze(2).broadcast_to((P, TB, E)),
                                ALU.is_equal).then_inc(hot_done, 1)

            def ranks(jb):
                dve.wait_ge(m_done, jb + 1)
                v.tensor_copy(rkc[:, :], m_ps[:, 0:2 * TB * E]).then_inc(m_free, 1)

            def places(jb, p):
                dve.wait_ge(m_free, jb + 1)
                rank = lambda t: rkc[:, t * E:(t + 1) * E]
                count = lambda t: rkc[:, (TB + t) * E:(TB + t + 1) * E]
                v.tensor_tensor(pos4[:, 0:E], rank(0), run[:, :], ALU.add)
                link(v.tensor_tensor(off1[:, :], run[:, :], count(0), ALU.add))
                v.tensor_tensor(pos4[:, E:2 * E], rank(1), off1[:, :], ALU.add)
                link(v.tensor_tensor(run[:, :], off1[:, :], count(1), ALU.add))
                link(v.tensor_tensor(pos4h[:, :], pos4[:, :], hot[:, :], ALU.mult))
                link(v.tensor_reduce(pos_f[:, :], by_expert(pos4h), AX.X, ALU.add))
                v.tensor_copy(pos_i[:, p * TB:(p + 1) * TB], pos_f[:, :]).then_inc(pos_done, 1)

            dve.wait_ge(x_in, 16)
            norm_a(0)
            norm_b(0)
            split_lo(SPLIT_FIRST[0])
            norm_c(0)
            split_lo(SPLIT_FIRST[1])
            split_lo(SPLIT_FIRST[2])
            dve.wait_ge(consts_in, 32)
            x_affine(0, job(-1, "px"))
            split_lo(SPLIT_FIRST[3])
            x_low(0, 0)
            ctx_low(0, 0)
            for c in SPLIT_THEN:
                split_lo(c)
            qk_low(0, 0)
            qk_low(1, 1)
            maxima(0, 0, 0)
            maxima(0, 0, 1)
            qk_low(2, 2)
            v_evacuate(job(-1, "v0a"), 0, 0)
            inverse_sums(0, 0, 0)
            inverse_sums(0, 0, 1)
            v_evacuate(job(-1, "v0b"), 0, 1)
            dve.wait_ge(gate_in, 64)
            dve.wait_ge(consts_set, 2)
            dve.wait_ge(x_rest_in, 16)
            base0 = chain["base"] + chain["n"]
            PER_BATCH = 3 + 1 + 4 + 4

            def body(b, p, b_half):
                first, last = is_first(b), is_last(b)
                chain["base"], chain["n"] = base0 if first else base0 + 3 + PER_BATCH * (b - 1), 0
                u0 = 8 * b
                for hp in range(HP):
                    u = u0 + hp
                    if hp == 3 and not last:
                        x_affine(b + 1, job(b, "px"))
                    if hp == 4:
                        if not last:
                            x_low(b + 1, 1 - p)
                    if hp == 5 and not first:
                        xf_evacuate(job(b, "tf"), B if last else b + 2)
                    if hp == 6 and not first:
                        logits(job(b, "lg"))
                    if not (first and hp < 2):
                        out_low(u - 2, p if hp >= 2 else 1 - p, (hp - 2) % HP)
                    if not (last and hp == HP - 1):
                        maxima(u + 1, (hp + 1) % 2, 0)
                        maxima(u + 1, (hp + 1) % 2, 1)
                    if hp == 1 and not last:
                        norm_a(b + 1)
                    if not last or hp + 3 < HP:
                        qk_low(u + 3, (hp + 3) % QS)
                    if hp == 0 and not last:
                        ctx_low(b + 1, 1 - p)
                    if not (last and hp == HP - 1):
                        inverse_sums(u + 1, (hp + 1) % 2, 0)
                    if hp in (3, 4):
                        v_evacuate(job(b, f"v1{'ab'[hp - 3]}"), 1, hp - 3)
                    if hp in (5, 6) and not last:
                        v_evacuate(job(b, f"v0{'ab'[hp - 5]}"), 0, hp - 5)
                    if hp == 7 and not first:
                        ranks(job(b, "rk"))
                    if not (last and hp == HP - 1):
                        inverse_sums(u + 1, (hp + 1) % 2, 1)
                    if hp in (1, 2) and not first:
                        residual(b - 1, 1 - p, b_half if p else b_half - 1, hp - 1, job(b, f"out{hp - 1}"))
                    if not last:
                        if hp == 1:
                            norm_b(b + 1)
                        if hp == 2:
                            norm_c(b + 1)
                    if not first:
                        if hp == 2:
                            ffn_norm_a(b - 1, 1 - p, job(b, "out1"))
                        if hp == 3:
                            ffn_norm_b(b - 1, 1 - p)
                        if hp == 6:
                            choose(job(b, "lg"))
                        if hp == 7:
                            places(job(b, "rk"), 1 - p)
                        if last and hp == 7:
                            v.tensor_copy(run_i[:, :], run[:, :]).then_inc(run_done, 1)
                assert chain["n"] == (3 if first else PER_BATCH - 3 if last else PER_BATCH)

            batches(body, dve)
            chain["base"], chain["n"] = base0 + 3 + PER_BATCH * (B - 2) + PER_BATCH - 3, 0
            out_low(B * HP - 2, 1, HP - 2)
            out_low(B * HP - 1, 1, HP - 1)

            def ffn_lo(lo, hi, c, hi_done, done):
                dve.wait_ge(hi_done, c + 1)
                v.tensor_tensor(ffn_chunk(lo, c), ffn_chunk(lo, c).bitcast(F32), ffn_chunk(hi, c).bitcast(F32),
                                ALU.subtract).then_inc(done, 1)

            rest = FCH - FCH_DVE
            for t in range(TB):
                residual(B - 1, 1, (B - 1) // 2, t, job(B, f"out{t}"), out_ps[t])
            v.memset(b2_b[:, 0:1], 0.0).then_inc(phase_a_left, 1)
            ffn_norm_a(B - 1, 1, job(B, "out1"))
            for c in range(rest, rest + 2):
                ffn_lo(w1_lo, w1_hi, c, f1_hi_done, f1_lo_done)
            ffn_norm_b(B - 1, 1)
            xf_evacuate(job(B, "tf"), B)
            for c in range(rest + 2, rest + 4):
                ffn_lo(w1_lo, w1_hi, c, f1_hi_done, f1_lo_done)
            logits(job(B, "lg"))
            choose(job(B, "lg"))
            ranks(job(B, "rk"))
            places(job(B, "rk"), 1)

            dve.wait_ge(consts_set, 3)
            link(v.tensor_tensor(n_f[:, :], run[:, :], reg0[:, :], ALU.subtract))
            link(v.tensor_scalar(n_f[:, :], n_f[:, :], float(P - 1), None, ALU.add))
            link(v.tensor_copy(n_i[:, :], n_f[:, :]))
            link(v.tensor_scalar(t_i[:, :], n_i[:, :], P.bit_length() - 1, None, ALU.arith_shift_right))
            link(v.tensor_copy(t_f[:, :], t_i[:, :]))
            v.tensor_scalar(skip[:, :], t_f[:, :], -float(P), float(REG), ALU.mult, ALU.add)
            link(v.tensor_tensor_scan(t_inc[:, :], ones_e[:, :], t_f[:, :], 0.0, ALU.mult, ALU.add))
            for e in range(E):
                s = slice(e * NG, (e + 1) * NG)
                if e < E - 1:
                    v.tensor_scalar(g_ge[:, s], g_io[:, :], t_inc[:, e:e + 1], None, ALU.is_ge)
                last = v.tensor_scalar(g_sk[:, s], g_io[:, :], t_inc[:, e:e + 1], skip[:, e:e + 1], ALU.is_ge, ALU.mult)
            link(last)
            v.tensor_tensor(g_ex[:, :], g_ge[:, 0:NG], g_ge[:, NG:2 * NG], ALU.add)
            v.scalar_tensor_tensor(out=g_row[:, :], in0=g_io[:, :], scalar=float(P), in1=g_sk[:, 0:NG],
                                   op0=ALU.mult, op1=ALU.add).then_inc(dve_chain, 1)
            chain["n"] += 1
            dve.wait_ge(dve_chain, chain["base"] + chain["n"])
            v.tensor_tensor(g_ex[:, :], g_ex[:, :], g_ge[:, 2 * NG:3 * NG], ALU.add)
            link(v.tensor_tensor(g_row[:, :], g_row[:, :], g_sk[:, NG:2 * NG], ALU.add))
            v.tensor_copy(g_i[:, :], g_ex[:, :])
            link(v.tensor_tensor(g_row[:, :], g_row[:, :], g_sk[:, 2 * NG:3 * NG], ALU.add))
            link(v.tensor_tensor(g_row[:, :], g_row[:, :], g_sk[:, 3 * NG:4 * NG], ALU.add))
            v.tensor_copy(g_r[:, :], g_row[:, :]).then_inc(plan_done, 1)

            for c in range(rest + 4, FCH):
                ffn_lo(w1_lo, w1_hi, c, f1_hi_done, f1_lo_done)
            for c in range(2):
                ffn_lo(w2_lo, w2_hi, c, f2_hi_done, f2_lo_done)

            dve.wait_ge(b1_in, 48)
            dve.wait_ge(plan_done, 1)

            def expert_of(n):
                return dve.value_load(g_i[0:1, n:n + 1] if isinstance(n, int) else g_i[0:1, bass.ds(n, 1)],
                                      min_val=0, max_val=E - 1)

            def h_bias(n, par, ex, c):
                dve.wait_ge(h_done, 2 * n + c + 1)
                col = par * F + c * CH
                v.tensor_tensor(h1[:, col:col + CH], h_ps[c][:, :],
                                b1_b[:, bass.ds(ex * F + c * CH, CH)], ALU.add).then_inc(h1_done, 1)

            def xg_low(n, par):
                dve.wait_ge(xgt_hi_done, n + 1)
                s = slice(par * DC * P, (par + 1) * DC * P)
                v.tensor_tensor(xgt_lo[:, s], xt_ps[par][:, 0:DC * P], xgt_hi[:, s].bitcast(F32),
                                ALU.subtract).then_inc(xgt_lo_done, 1)

            def ht_low(n, par, c):
                dve.wait_ge(h1t_hi_done, 2 * n + c + 1)
                s = slice(par * F + c * CH, par * F + (c + 1) * CH)
                v.scalar_tensor_tensor(out=h1t_lo[:, s], in0=ht_ps[c][:, :], scalar=0.0,
                                       in1=h1t_hi[:, s].bitcast(F32), op0=ALU.max,
                                       op1=ALU.subtract).then_inc(h1t_lo_done, 1)

            def tile_norm(n, par, n_half):
                dve.wait_ge(xg_in[par], 16 * (n_half + 1))
                wait(dve, xgt_ps_done, n - 1)
                c = par * RW
                v.tensor_scalar(xfg[:, par * D:(par + 1) * D], xg[:, c:c + D], xg[:, c + D:c + D + 1],
                                xg[:, c + D + 1:c + D + 2], ALU.subtract, ALU.mult).then_inc(xfg_done, 1)

            def y_add(n, par, n_half):
                dve.wait_ge(y_done, n + 1)
                dve.wait_ge(xb2_done, n + 1)
                wait(dve, stored[par], 16 * n_half)
                v.tensor_tensor(y_sb[:, par * D:(par + 1) * D], y_ps[par][:, 0:D],
                                xb2[:, par * D:(par + 1) * D], ALU.add).then_inc(ysb_done, 1)

            tile_norm(0, 0, 0)
            tile_norm(1, 1, 0)
            xg_low(0, 0)
            xg_low(1, 1)
            ex = expert_of(0)
            for c in range(2, 4):
                ffn_lo(w2_lo, w2_hi, c, f2_hi_done, f2_lo_done)
            h_bias(0, 0, ex, 0)
            for c in range(4, FCH - FCH_POOL):
                ffn_lo(w2_lo, w2_hi, c, f2_hi_done, f2_lo_done)
            h_bias(0, 0, ex, 1)

            def step(n, par, n_half, last):
                two_ahead = not (last or isinstance(n, int) and n + 2 >= NG)
                if two_ahead:
                    tile_norm(n + 2, par, n_half + 1)
                if not last:
                    nxt = expert_of(n + 1)
                    h_bias(n + 1, 1 - par, nxt, 0)
                ht_low(n, par, 0)
                ht_low(n, par, 1)
                if two_ahead:
                    xg_low(n + 2, par)
                if not last:
                    h_bias(n + 1, 1 - par, nxt, 1)
                y_add(n, par, n_half)

            expert_tiles(step, dve)

        @block.tensor
        def _(pe):
            mm = nc.tensor.matmul

            def three(outp, terms, first=True, final=True):
                n = len(terms)
                for k, (lh, ll, rh, rl) in enumerate(terms):
                    mm(outp, lh, rh, start=first and k == 0, stop=False)
                    mm(outp, lh, rl, start=False, stop=False)
                    last = mm(outp, ll, rh, start=False, stop=final and k == n - 1)
                return last

            def project_qk(u, hp, par):
                wait(pe, qk_lo, u - 1)
                bank = qk_ps[hp % 2]
                s = [slice((par * DC + c) * S, (par * DC + c + 1) * S) for c in range(DC)]
                three(bank[:, 0:S], [(wq_ap(w_hi, c, hp), wq_ap(w_lo, c, hp), xt_hi[:, s[c]], xt_lo[:, s[c]])
                                      for c in range(DC)])
                three(bank[:, S:2 * S], [(wk_ap(w_hi, c, hp), wk_ap(w_lo, c, hp), ct_hi[:, s[c]], ct_lo[:, s[c]])
                                          for c in range(DC)]).then_inc(qk_done, 1)

            def project_v(jb, hf, kt, par):
                wait(pe, m_free, jb)
                s = [slice((par * DC + c) * S + kt * P, (par * DC + c) * S + (kt + 1) * P) for c in range(DC)]
                three(m_ps[:, :], [(ct_hi[:, s[c]], ct_lo[:, s[c]], wv_ap(w_hi, c, hf), wv_ap(w_lo, c, hf))
                                       for c in range(DC)]).then_inc(m_done, 1)

            def transposes(jb, src):
                wait(pe, m_free, jb)
                for t in range(TB):
                    for c in range(DC):
                        last = nc.tensor.transpose(m_ps[:, c * S + t * P:c * S + (t + 1) * P],
                                                   src[:, t * D + c * P:t * D + (c + 1) * P], ident[:, :])
                last.then_inc(m_done, 1)

            def scores(u, slot, j):
                wait(pe, exp_done, 2 * (u - 1) + j + 1)
                for t in range(TB):
                    q = qst(slot, j)[:, t * P:(t + 1) * P]
                    mm(s_ps[j][:, t * S:(t + 1) * S], q, kmv(slot, j, 0), start=True, stop=False)
                    last = mm(s_ps[j][:, t * S:(t + 1) * S], q, kmv(slot, j, 1), start=False, stop=True)
                last.then_inc(s_done, 1)

            def transpose_p(u, par, j):
                pe.wait_ge(norm_done, 2 * u + j + 1)
                wait(pe, pt_done, 2 * (u - 1) + j + 1)
                slot = 2 * par + j
                for t in range(TB):
                    for kt in range(TB):
                        c = (slot * TB + t) * S + kt * P
                        last = nc.tensor.transpose(t_ps[j][:, kt * S + t * P:kt * S + (t + 1) * P],
                                                   p_sb[:, c:c + P], ident[:, :])
                last.then_inc(t_done, 1)

            def attend(u, hp):
                wait(pe, pt_done, 2 * u + 2)
                wait(pe, ol_done, u)
                hf, q4 = hp // 4, hp % 4
                for kt in range(TB):
                    for j in range(2):
                        c = (hf * TB + kt) * CH + q4 * P + j * DH
                        last = mm(o_ps[half(j), 0:S], v_sb[:, c:c + DH],
                                  pt_sb[:, (j * TB + kt) * S:(j * TB + kt + 1) * S],
                                  start=(kt == 0), stop=(kt == TB - 1))
                last.then_inc(pv_done, 1)

            def project_out_pairs(bank, t, p, a, z):
                terms = []
                for hp in range(a, z):
                    s = slice(o_cols(p, hp) + t * P, o_cols(p, hp) + (t + 1) * P)
                    terms.append((o_hi[:, s], o_lo[:, s], wo_ap(wo_hi, hp), wo_ap(wo_lo, hp)))
                return three(bank[:, 0:D], terms, first=(a == 0), final=(z == HP))

            def project_out(jb, t, p):
                wait(pe, m_free, jb)
                project_out_pairs(m_ps, t, p, 0, HP).then_inc(m_done, 1)

            def router(jb):
                wait(pe, m_free, jb)
                for t in range(TB):
                    for c in range(DC):
                        last = mm(m_ps[:, t * E:(t + 1) * E], xt_f[:, c * S + t * P:c * S + (t + 1) * P],
                                  wr_c[:, c * E:(c + 1) * E], start=(c == 0), stop=(c == DC - 1))
                last.then_inc(m_done, 1)

            def rank(b, jb):
                wait(pe, m_free, jb)
                pe.wait_ge(hot_done, b + 1)
                mm(m_ps[:, 0:TB * E], upper[:, :], hot[:, :], start=True, stop=True)
                mm(m_ps[:, TB * E:2 * TB * E], ones_pp[:, :], hot[:, :], start=True, stop=True).then_inc(m_done, 1)

            pe.wait_ge(consts_set, 2)
            pe.wait_ge(xn_done, 1)
            transposes(job(-1, "px"), xn[:, :])
            pe.wait_ge(c_sem, 16)
            transposes(job(-1, "pc"), c_in[:, :])
            pe.wait_ge(wlo_done, len(SPLIT_FIRST))
            pe.wait_ge(xt_done, 1)
            pe.wait_ge(m_free, 2)
            for u in range(AHEAD - 1):
                project_qk(u, u, 0)
            pe.wait_ge(dup_done[0], 32)
            scores(0, 0, 0)
            scores(0, 0, 1)
            pe.wait_ge(vo_lo_done, CO - CV)
            project_v(job(-1, "v0a"), 0, 0, 0)
            project_qk(AHEAD - 1, AHEAD - 1, 0)
            project_v(job(-1, "v0b"), 0, 1, 0)
            pe.wait_ge(wlo_done, CV)
            pe.wait_ge(gate_in, 64)

            def body(b, p, b_half):
                first, last = is_first(b), is_last(b)

                def next_context():
                    pe.wait_ge(c_sem, 16 * (b + 2))
                    transposes(job(b, "pc"), c_in[:, :])

                for hp in range(HP):
                    u = 8 * b + hp
                    if hp == 3 and not last:
                        pe.wait_ge(xn_done, b + 2)
                        transposes(job(b, "px"), xn[:, :])
                    if hp == 0 and not (first or last):
                        next_context()
                    if not first:
                        if hp == 5:
                            pe.wait_ge(xf_done, b)
                            transposes(job(b, "tf"), xf[:, :])
                        if hp == 6:
                            router(job(b, "lg"))
                    if not (first and hp == 0):
                        transpose_p(u - 1, (hp + 1) % 2, 0)
                        transpose_p(u - 1, (hp + 1) % 2, 1)
                    if not (last and hp == HP - 1):
                        slot = (hp + 1) % QS
                        pe.wait_ge(dup_done[slot], 32 * (b * (HP // QS) + (hp + 1) // QS + 1))
                        scores(u + 1, slot, 0)
                        scores(u + 1, slot, 1)
                    if hp == 0 and first:
                        next_context()
                    if hp == 2 and not first:
                        project_out(job(b, "out1"), 1, 1 - p)
                    if hp == 7 and not first:
                        rank(b - 1, job(b, "rk"))
                    if hp in (3, 4):
                        project_v(job(b, f"v1{'ab'[hp - 3]}"), 1, hp - 3, p)
                    if hp in (5, 6) and not last:
                        project_v(job(b, f"v0{'ab'[hp - 5]}"), 0, hp - 5, 1 - p)
                    if hp == 1:
                        pe.wait_ge(m_free, job(b - 1, "v0b") + 1)
                    if hp == 5:
                        pe.wait_ge(m_free, job(b, "v1b") + 1)
                    if not (first and hp == 0):
                        attend(u - 1, (hp - 1) % HP)
                    if hp == 1 and not first:
                        pe.wait_ge(ol_done, u - 1)
                        pe.wait_ge(vo_lo_done, WCH - CV)
                        project_out(job(b, "out0"), 0, 1 - p)
                    if not last or hp + AHEAD < HP:
                        nxt = hp + AHEAD >= HP
                        if hp + AHEAD == HP:
                            pe.wait_ge(xt_done, b + 2)
                            pe.wait_ge(m_free, job(b, "pc") + 1)
                        project_qk(u + AHEAD, (hp + AHEAD) % HP, (1 - p) if nxt else p)

            batches(body, pe)
            for j in range(2):
                transpose_p(B * HP - 1, 1, j)
            pe.wait_ge(m_free, job(B, "out0"))
            pe.wait_ge(qk_lo, B * HP)
            pe.wait_ge(ol_done, B * HP - 2)
            for t in range(TB):
                project_out_pairs(out_ps[t], t, 1, 0, HP - 2)
            attend(B * HP - 1, HP - 1)
            for t in range(TB):
                project_out_pairs(out_ps[t], t, 1, HP - 2, HP - 1)
            pe.wait_ge(ol_done, B * HP)
            for t in range(TB):
                project_out_pairs(out_ps[t], t, 1, HP - 1, HP).then_inc(m_done, 1)

            pe.wait_ge(xf_done, B)
            transposes(job(B, "tf"), xf[:, :])
            router(job(B, "lg"))
            rank(B - 1, job(B, "rk"))

            def expert_of(n):
                return pe.value_load(g_i[0:1, n:n + 1] if isinstance(n, int) else g_i[0:1, bass.ds(n, 1)],
                                     min_val=0, max_val=E - 1)

            def x_in_tile(n, par):
                pe.wait_ge(xfg_done, n + 1)
                wait(pe, xgt_lo_done, n - 1)
                for c in range(DC):
                    last = nc.tensor.transpose(xt_ps[par][:, c * P:(c + 1) * P],
                                               xfg[:, par * D + c * P:par * D + (c + 1) * P], ident[:, :])
                last.then_inc(xgt_ps_done, 1)

            def up(n, par, ex, c):
                pe.wait_ge(xgt_lo_done, n + 1)
                wait(pe, h1_done, 2 * (n - 1) + c + 1)
                terms = []
                for k in range(DC):
                    s = slice((par * DC + k) * P, (par * DC + k + 1) * P)
                    cols = bass.ds(ex * (DC * F) + (k * F + c * CH), CH)
                    terms.append((xgt_hi[:, s], xgt_lo[:, s], w1_hi[:, cols], w1_lo[:, cols]))
                three(h_ps[c][:, :], terms).then_inc(h_done, 1)

            def hidden_t(n, par):
                for c in range(2):
                    pe.wait_ge(h1_done, 2 * n + c + 1)
                    for k in range(CH // P):
                        col = par * F + c * CH + k * P
                        last = nc.tensor.transpose(ht_ps[c][:, k * P:(k + 1) * P], h1[:, col:col + P], ident[:, :])
                    last.then_inc(ht_done, 1)

            def down(n, par, ex):
                if isinstance(n, int) and n == 0:
                    pe.wait_ge(f2_lo_done, FCH)
                for c in range(2):
                    pe.wait_ge(h1t_lo_done, 2 * n + c + 1)
                    terms = []
                    for k in range(c * FC // 2, (c + 1) * FC // 2):
                        s = slice(par * F + k * P, par * F + (k + 1) * P)
                        cols = bass.ds(ex * (FC * D) + k * D, D)
                        terms.append((h1t_hi[:, s], h1t_lo[:, s], w2_hi[:, cols], w2_lo[:, cols]))
                    last = three(y_ps[par][:, 0:D], terms, first=(c == 0), final=(c == 1))
                last.then_inc(y_done, 1)

            pe.wait_ge(plan_done, 1)
            pe.wait_ge(f1_lo_done, FCH)
            x_in_tile(0, 0)
            x_in_tile(1, 1)
            expert = {"next": expert_of(0)}
            for c in range(2):
                up(0, 0, expert["next"], c)

            def step(n, par, n_half, last):
                other_block = par == 0 and not isinstance(n, int) or isinstance(n, int) and n == NG - 3
                this = None if other_block else expert["next"]
                if not last:
                    expert["next"] = nxt = expert_of(n + 1)
                    up(n + 1, 1 - par, nxt, 0)
                hidden_t(n, par)
                if not (last or isinstance(n, int) and n + 2 >= NG):
                    x_in_tile(n + 2, par)
                if not last:
                    up(n + 1, 1 - par, nxt, 1)
                down(n, par, expert_of(n) if other_block else this)

            expert_tiles(step, pe)


def kernel(x, ctx_1024, L0_xattn_ln_gamma, L0_xattn_ln_beta, L0_xattn_w_q, L0_xattn_w_kv, L0_xattn_w_out,
           L0_xattn_b_out, L0_xattn_gate, L0_ffn_Wr, L0_ffn_br, L0_ffn_We1, L0_ffn_be1, L0_ffn_We2, L0_ffn_be2):
    import numpy as np
    import concourse.bacc as bacc
    from concourse.bass_utils import run_bass_kernel_spmd

    ins = {
        "x": x, "ctx": ctx_1024,
        "ln_gamma": np.asarray(L0_xattn_ln_gamma).reshape(DC, P).T, "ln_beta": np.asarray(L0_xattn_ln_beta).reshape(DC, P).T,
        "w_q": L0_xattn_w_q, "w_kv": L0_xattn_w_kv, "w_out": L0_xattn_w_out, "b_out": L0_xattn_b_out,
        "gate": L0_xattn_gate, "w_router": L0_ffn_Wr, "b_router": L0_ffn_br,
        "we1": L0_ffn_We1, "be1": L0_ffn_be1, "we2": L0_ffn_We2, "be2": L0_ffn_be2,
    }
    nc = bacc.Bacc("TRN2", target_bir_lowering=False, num_devices=1)
    arrays, args = {}, []
    for name, a in ins.items():
        a = np.ascontiguousarray(a)
        arrays["in_" + name] = a
        args.append(nc.dram_tensor("in_" + name, a.shape, mybir.dt.from_np(a.dtype), kind="ExternalInput").ap())
    args.append(nc.dram_tensor("out_x", (B, S, D), F32, kind="ExternalOutput").ap())
    attention_and_routed_ffn(nc, *args)
    r = run_bass_kernel_spmd(nc, [arrays], core_ids=[0])
    return r.results[0]["out_x"]
```
